# Optimizing a Trainium2 kernel written in Bass

```python
import numpy as np
import jax
import jax.numpy as jnp

def _softmax(x, axis=-1):
    return jax.nn.softmax(x, axis=axis)

def _gelu(x):
    return jax.nn.gelu(x, approximate=True)

def _silu(x):
    return jax.nn.silu(x)

def _sigmoid(x):
    return jax.nn.sigmoid(x)

def _layernorm(x, axis=-1, eps=1e-05):
    m = jnp.mean(x, axis=axis, keepdims=True)
    v = jnp.var(x, axis=axis, keepdims=True)
    return (x - m) / jnp.sqrt(v + eps)

def _scatter_add(tgt, idx, src, axis=0):
    return tgt.at[idx].add(src)

def _segment_sum(src, seg, n):
    return jax.ops.segment_sum(src, seg, n)
kernel_name = 'mk_macaron_d1_jaxref_r8_60d043'

def setup_inputs(seed: int=0):
    np.random.seed(seed)
    _w = jnp.asarray

    def _L0_attn_setup():
        import jax, jax.numpy as jnp
        import numpy as np
        B, N, DIM = (2, 256, 256)
        HEADS, DIM_HEAD, GQA = (16, 64, 4)
        KV_HEADS = HEADS // GQA
        DIM_INNER = HEADS * DIM_HEAD
        KV_INNER = KV_HEADS * DIM_HEAD
        THETA = 10000.0

        def _rotate_half(t):
            t1, t2 = jnp.split(t, 2, axis=-1)
            return jnp.concatenate([-t2, t1], axis=-1)
        key = jax.random.key(seed)
        k1, k2, k3 = jax.random.split(key, 3)
        x = jax.random.normal(k1, (B, N, DIM), dtype=jnp.float32)
        gamma = jnp.ones((DIM,), dtype=jnp.float32)
        w_qkv = jax.random.normal(k2, (DIM, DIM_INNER + 2 * KV_INNER), dtype=jnp.float32) * DIM ** (-0.5)
        w_out = jax.random.normal(k3, (DIM_INNER, DIM), dtype=jnp.float32) * DIM_INNER ** (-0.5)
        return {'x': x, 'gamma': gamma, 'w_qkv': w_qkv, 'w_out': w_out}
    _L0_attn_in = _L0_attn_setup()

    def _L0_ffn_setup():
        import jax, jax.numpy as jnp
        import numpy as np
        DIM_IN = 256
        DIM_HIDDEN = 1024
        key = jax.random.key(seed)
        k_x, k_g, k_u, k_d = jax.random.split(key, 4)
        s_in = 1.0 / np.sqrt(DIM_IN)
        s_hid = 1.0 / np.sqrt(DIM_HIDDEN)
        x = jax.random.normal(k_x, (4, 256, DIM_IN), dtype=jnp.float32)
        w_gate = jax.random.uniform(k_g, (DIM_HIDDEN, DIM_IN), jnp.float32, -s_in, s_in)
        w_up = jax.random.uniform(k_u, (DIM_HIDDEN, DIM_IN), jnp.float32, -s_in, s_in)
        w_down = jax.random.uniform(k_d, (DIM_IN, DIM_HIDDEN), jnp.float32, -s_hid, s_hid)
        return {'x': x, 'w_gate': w_gate, 'w_up': w_up, 'w_down': w_down}
    _L0_ffn_in = _L0_ffn_setup()
    _d = {'L0_attn_x': _L0_attn_in['x'], 'L0_attn_gamma': _L0_attn_in['gamma'], 'L0_attn_w_qkv': _L0_attn_in['w_qkv'], 'L0_attn_w_out': _L0_attn_in['w_out'], 'L0_ffn_w_gate': _L0_ffn_in['w_gate'], 'L0_ffn_w_up': _L0_ffn_in['w_up'], 'L0_ffn_w_down': _L0_ffn_in['w_down']}
    _x0 = _d['L0_attn_x']
    _d['L0_attn_x'] = jax.random.normal(jax.random.fold_in(jax.random.key(seed), 1), (8, 256, 256), dtype=_x0.dtype)
    del _x0
    return _d

def reference(L0_attn_x, L0_attn_gamma, L0_attn_w_qkv, L0_attn_w_out, L0_ffn_w_gate, L0_ffn_w_up, L0_ffn_w_down):

    def _L0_attn_ref(x, gamma, w_qkv, w_out):
        import jax, jax.numpy as jnp
        import numpy as np
        B, N, DIM = (2, 256, 256)
        HEADS, DIM_HEAD, GQA = (16, 64, 4)
        KV_HEADS = HEADS // GQA
        DIM_INNER = HEADS * DIM_HEAD
        KV_INNER = KV_HEADS * DIM_HEAD
        THETA = 10000.0

        def _rotate_half(t):
            t1, t2 = jnp.split(t, 2, axis=-1)
            return jnp.concatenate([-t2, t1], axis=-1)
        b, n, _ = x.shape
        norm = jnp.linalg.norm(x, axis=-1, keepdims=True)
        x_n = x / jnp.maximum(norm, 1e-12) * DIM ** 0.5 * gamma
        qkv = (x_n @ w_qkv).reshape(b, n, HEADS + 2 * KV_HEADS, DIM_HEAD)
        q = qkv[..., :HEADS, :]
        k = qkv[..., HEADS:HEADS + KV_HEADS, :]
        v = qkv[..., HEADS + KV_HEADS:, :]
        pos = jnp.arange(n, dtype=jnp.float32)
        inv_freq = THETA ** (-(jnp.arange(0, DIM_HEAD, 2, dtype=jnp.float32) / DIM_HEAD))
        freqs = pos[:, None] * inv_freq[None, :]
        rot = jnp.concatenate([freqs, freqs], axis=-1)[:, None, :]
        cos, sin = (jnp.cos(rot), jnp.sin(rot))
        q = q * cos + _rotate_half(q) * sin
        k = k * cos + _rotate_half(k) * sin
        k = jnp.tile(k, (1, 1, GQA, 1))
        v = jnp.tile(v, (1, 1, GQA, 1))
        q = q * DIM_HEAD ** (-0.5)
        sim = jnp.einsum('bihd,bjhd->bhij', q, k)
        causal_mask = jnp.triu(jnp.ones((n, n), dtype=bool), 1)
        sim = jnp.where(causal_mask, -jnp.finfo(sim.dtype).max, sim)
        attn = jax.nn.softmax(sim, axis=-1)
        out = jnp.einsum('bhij,bjhd->bihd', attn, v)
        out = out.reshape(b, n, DIM_INNER)
        return out @ w_out

    def _L0_ffn_ref(x, w_gate, w_up, w_down):
        import jax, jax.numpy as jnp
        import numpy as np
        DIM_IN = 256
        DIM_HIDDEN = 1024
        gate = jnp.einsum('bsd,hd->bsh', x, w_gate)
        up = jnp.einsum('bsd,hd->bsh', x, w_up)
        gated = jax.nn.silu(gate) * up
        return jnp.einsum('bsh,dh->bsd', gated, w_down)
    x = L0_attn_x
    x = x + 0.5 * _L0_ffn_ref(_layernorm(x, axis=-1), L0_ffn_w_gate, L0_ffn_w_up, L0_ffn_w_down)
    x = x + _L0_attn_ref(_layernorm(x, axis=-1), L0_attn_gamma, L0_attn_w_qkv, L0_attn_w_out)
    x = x + 0.5 * _L0_ffn_ref(_layernorm(x, axis=-1), L0_ffn_w_gate, L0_ffn_w_up, L0_ffn_w_down)
    return x

_drawn_inputs = setup_inputs


def setup_inputs(seed=0):
    import zlib

    import numpy as np

    out = dict(_drawn_inputs(seed))
    spreads = {'L0_attn_gamma': (1.0, 0.2)}
    factors = {}
    for name, (base, spread) in spreads.items():
        noise = np.random.default_rng([zlib.crc32(name.encode()), seed]).standard_normal(out[name].shape)
        drawn = base * np.exp(spread * noise) if base else spread * noise
        out[name] = jnp.asarray(drawn.astype(out[name].dtype))
    for name, factor in factors.items():
        out[name] = (out[name] * factor).astype(out[name].dtype)
    return out
```

```python
import numpy as np
import concourse.bass as bass
from concourse import mybir
from contextlib import ExitStack

F32 = mybir.dt.float32
F32R = mybir.dt.float32r
ALU = mybir.AluOpType
ACT = mybir.ActivationFunctionType

BATCH, SEQ, DIM = 8, 256, 256
HEADS, KV_HEADS, DH = 16, 4, 64
GROUP = HEADS // KV_HEADS
HID = 1024
P = 128
NT = SEQ // P
KC = DIM // P
QKV = (HEADS + 2 * KV_HEADS) * DH
PAIRS = HID // (2 * P)
OC = HEADS * DH // P
MASKED = -3.0e38
EPS = 1e-5
NORM_MIN = 1e-12
GROUPS = NT * KV_HEADS
P_JOBS = KV_HEADS * (1 + NT)


def key_blocks(n):
    return n // KV_HEADS + 1


class Turn:

    def __init__(self, per_turn):
        self.per_turn, self.now = per_turn, None

    def at(self, semaphore, count):
        if self.now is None:
            return max(count, 0)
        per_turn = self.per_turn[semaphore.name]
        assert count > 0 and per_turn
        return (self.now - 1) * per_turn + count

    def apart(self, engine, semaphore, count):
        value = self.at(semaphore, count)
        return value if self.now is None else engine.to_reg(value)


def tally(**kinds):
    return {kind: 0 for kind in kinds}


def after_loop(c, before, per_turn, turns):
    for kind, n in per_turn.items():
        assert c[kind] - before[kind] == n, (kind, c[kind] - before[kind])
        c[kind] += (turns - 1) * n


JOBS = dict(T=3 + 6 + P_JOBS, Q=6, S=GROUPS, OT=2 * NT, Y=NT, F=2 * PAIRS, D=2, LN=3, X=1)


def build(nc, x, w_gate, w_up, w_down, w_qkv, w_out, gamma, rope, mask, eye, out):
    ctx = ExitStack()
    with ctx:
        def sb(name, shape, dt=F32):
            return ctx.enter_context(nc.sbuf_tensor(name, shape, dt))

        raised = {}

        def sig(name, per_turn=0):
            semaphore = ctx.enter_context(nc.semaphore(name))
            raised[semaphore.name] = per_turn
            return semaphore

        gate_w = [sb(f"gate_{s}", [P, KC, HID], F32R) for s in ("hi", "lo")]
        up_w = [sb(f"up_{s}", [P, KC, HID], F32R) for s in ("hi", "lo")]
        down_w = [sb(f"down_{s}", [P, HID // P, DIM], F32R) for s in ("hi", "lo")]
        qkv_w = [sb(f"qkv_{s}", [P, KC, QKV], F32R) for s in ("hi", "lo")]
        out_w = [sb(f"out_{s}", [P, OC, DIM], F32R) for s in ("hi", "lo")]
        gamma_sb = sb("gamma_sb", [P, KC])
        rope_sb = sb("rope_sb", [P, NT, 2, DH])
        mask_sb = sb("mask_sb", [P, SEQ])
        eye_sb = sb("eye_sb", [P, P])
        exponent = sb("exponent", [P, 2, NT])

        x_in = sb("x_in", [P, NT, DIM])
        x1_next = sb("x1_next", [P, NT, DIM])
        x1 = sb("x1", [P, NT, DIM])
        x2 = sb("x2", [P, NT, DIM])
        xn = sb("xn", [P, NT, DIM])
        xf_t = [sb(f"xf_t_{s}", [P, KC, SEQ], F32R) for s in ("hi", "lo")]
        xa_t = [sb(f"xa_t_{s}", [P, KC, SEQ], F32R) for s in ("hi", "lo")]
        stats = sb("stats", [P, NT, 6])
        mean_var = sb("mean_var", [P, NT, 2])
        power_in = sb("power_in", [P, 2, NT])
        power_out = sb("power_out", [P, 2, NT])
        factor = sb("factor", [P, NT])

        hid = sb("hid", [P, 2, 2 * P * NT])
        hid_hi = sb("hid_hi", [P, 2, 2, SEQ], F32R)
        hid_lo = sb("hid_lo", [P, 2, 2, SEQ], F32R)

        rope_c = sb("rope_c", [P, 2, 8, DH])
        rope_s = sb("rope_s", [P, 2, 8, DH])
        q_rot = sb("q_rot", [P, 2, 8 * DH])
        k_rot = sb("k_rot", [P, KV_HEADS, 2, DH])
        q_t = sb("q_t", [P, NT, HEADS, P], F32R)
        k_t = [sb(f"k_t_{s}", [P, KV_HEADS, SEQ], F32R) for s in ("hi", "lo")]
        v_pad = [sb(f"v_pad_{s}", [P, NT, 2, 3 * DH], F32R) for s in ("hi", "lo")]
        probs = sb("probs", [P, 4, GROUP, SEQ])
        row_max = sb("row_max", [P, 4, GROUP])
        neg_max = sb("neg_max", [P, 4, GROUP])
        row_sum = sb("row_sum", [P, 4, GROUP])
        inv_sum = sb("inv_sum", [P, 4, GROUP])
        p_t = [sb(f"p_t_{s}", [P, NT, GROUP * P], F32R) for s in ("hi", "lo")]
        o_t = [sb(f"o_t_{s}", [P, NT, 2, GROUP, P], F32R) for s in ("hi", "lo")]

        bank = [ctx.enter_context(nc.psum_tensor(f"bank{i}", [P, 512], F32)) for i in range(8)]
        Q_BANKS, S_BANKS, Y_BANKS, T_BANKS = (0, 1, 4), (0, 1), (0, 1), (2, 3)
        O_BANK, G_BANK, U_BANK, D_BANK = 4, 5, 6, 7
        Q_T_BANK = ((3, 2, 3), (3, 2, 3))
        F2_BANK, F1_BANK, XA_BANK = 2, 2, 3

        def p_bank(n, kb):
            before = min(n, KV_HEADS) + 2 * max(n - KV_HEADS, 0) + kb
            return T_BANKS[(before + 1) % 2]

        eye_in, gamma_in, tables_in = sig("eye_in"), sig("gamma_in"), sig("tables_in")
        w_in = [sig(f"w_in{i}") for i in range(4)]
        w_hi, w_lo = sig("w_hi"), sig("w_lo")
        pads_zero = sig("pads_zero")
        x_loaded = sig("x_loaded", 16)
        x_sent = sig("x_sent", 16)
        x1_kept = sig("x1_kept", 1)
        ln_var = sig("ln_var", JOBS["LN"])
        ln_pow = sig("ln_pow", JOBS["LN"])
        xn_ready = sig("xn_ready", JOBS["LN"])
        t_ready, t_hi, t_lo = (sig(n, JOBS["T"]) for n in ("t_ready", "t_hi", "t_lo"))
        q_ready = sig("q_ready", 6)
        rope_mul, rope_sum = sig("rope_mul", 6), sig("rope_sum", 6)
        v_done = sig("v_done", NT)
        s_ready, s_used = sig("s_ready", 2 * GROUPS), sig("s_used", 2 * GROUPS)
        s_max, e_done, r_done, p_done = (sig(n, GROUPS) for n in ("s_max", "e_done", "r_done", "p_done"))
        o_ready, o_hi, o_lo = (sig(n, JOBS["OT"]) for n in ("o_ready", "o_hi", "o_lo"))
        y_ready, y_used = sig("y_ready", NT), sig("y_used", NT)
        g_ready, u_ready, th_done, gate_used, mul_done, h_hi, h_lo, dn_done = (
            sig(n, JOBS["F"]) for n in
            ("g_ready", "u_ready", "th_done", "gate_used", "mul_done", "h_hi", "h_lo", "dn_done"))
        d_used = sig("d_used", JOBS["D"])
        DVE_OWN = 3 * 2 + 4 + NT
        dve_own = sig("dve_own", DVE_OWN)

        pieces = []
        for w, dst, name in ((w_gate, gate_w, "gate"), (w_up, up_w, "up")):
            pieces += [(w[:, k, :], [d[:, k, :] for d in dst], None) for k in range(KC)]
        half = HID // P // 2
        pieces += [(w_down[:, half * i:half * i + half, :].rearrange("p c n -> p (c n)"),
                    [d[:, half * i:half * i + half, :].rearrange("p c n -> p (c n)") for d in down_w], None)
                   for i in range(2)]
        pieces += [(w_qkv[:, k, i:i + QKV // 2], [d[:, k, i:i + QKV // 2] for d in qkv_w], k)
                   for k in range(KC) for i in (0, QKV // 2)]
        pieces += [(w_out[:, half * i:half * i + half, :].rearrange("p c n -> p (c n)"),
                    [d[:, half * i:half * i + half, :].rearrange("p c n -> p (c n)") for d in out_w], None)
                   for i in range(2)]
        W_GATE_UP, W_DOWN, W_ALL = 2 * KC, 2 * KC + 2, len(pieces)

        def stage(i):
            n = pieces[i][0].shape[1]
            return probs[:, i % 4].rearrange("p g k -> p (g k)")[:, 0:n]

        block = ctx.enter_context(nc.Block())

        @block.sync
        def _(sp):
            turn = Turn(raised)

            def load_x(m):
                sp.dma_start(x_in[:], x[bass.ds(m, 1)].rearrange("o (t p) d -> p (o t) d", p=P)
                             ).then_inc(x_loaded, 16)

            def store(m):
                sp.dma_start(out[bass.ds(m, 1)].rearrange("o (t p) d -> p (o t) d", p=P), x2[:]
                             ).then_inc(x_sent, 16)

            load_x(0)
            sp.dma_start(eye_sb[:], eye).then_inc(eye_in, 16)
            sp.dma_start(gamma_sb[:], gamma).then_inc(gamma_in, 16)
            for i, (src, _, _) in enumerate(pieces):
                if i >= 4:
                    sp.wait_ge(w_lo, turn.at(w_lo, i - 3))
                sp.dma_start(stage(i), src).then_inc(w_in[i % 4], 16)
                if i == W_GATE_UP:
                    sp.dma_start(rope_sb[:], rope).then_inc(tables_in, 16)
                    sp.dma_start(mask_sb[:], mask).then_inc(tables_in, 16)
            sp.wait_ge(d_used, turn.at(d_used, 1))
            load_x(1)
            with sp.Fori(1, BATCH - 1) as turn.now:
                sp.wait_ge(d_used, turn.at(d_used, 2))
                load_x(turn.now + 1)
                sp.wait_ge(d_used, turn.at(d_used, 3))
                store(turn.now - 1)
            turn.now = None
            n = 2 + 2 * (BATCH - 2)
            sp.wait_ge(d_used, turn.at(d_used, n + 1))
            store(BATCH - 2)
            sp.wait_ge(d_used, turn.at(d_used, n + 2))
            store(BATCH - 1)
            sp.wait_ge(x_sent, turn.at(x_sent, 16 * BATCH))

        @block.gpsimd
        def _(pool):
            turn, per_turn = Turn(raised), dict(T=JOBS["T"], Q=JOBS["Q"], S=JOBS["S"], F=JOBS["F"], LN=JOBS["LN"])
            c = tally(**per_turn)
            for v in v_pad:
                nc.gpsimd.memset(v[:].bitcast(F32), 0.0).then_inc(pads_zero, 1)
            nc.gpsimd.memset(exponent[:, 0], -0.5).then_inc(pads_zero, 1)
            nc.gpsimd.memset(exponent[:, 1], 0.5).then_inc(pads_zero, 1)
            pool.wait_ge(pads_zero, turn.at(pads_zero, 4))

            def powers():
                pool.wait_ge(ln_var, turn.at(ln_var, c["LN"] + 1))
                nc.gpsimd.tensor_tensor(power_out[:], power_in[:], exponent[:], ALU.pow
                                        ).then_inc(ln_pow, 1)
                c["LN"] += 1

            def rope_add(t, i):
                slot = c["Q"] % 2
                pool.wait_ge(rope_mul, turn.at(rope_mul, c["Q"] + 1))
                pool.wait_ge(t_ready, turn.at(t_ready, c["T"] + i + 1 if t else c["T"]))
                if i < 2:
                    nc.gpsimd.tensor_tensor(
                        q_rot[:, i], rope_c[:, slot].rearrange("p h d -> p (h d)"),
                        rope_s[:, slot].rearrange("p h d -> p (h d)"), ALU.add).then_inc(rope_sum, 1)
                else:
                    for copy in range(2):
                        last = nc.gpsimd.tensor_tensor(
                            k_rot[:, :, copy, :], rope_c[:, slot, 0:KV_HEADS],
                            rope_s[:, slot, 0:KV_HEADS], ALU.add)
                    last.then_inc(rope_sum, 1)
                c["Q"] += 1

            def normalise():
                slot, keys = c["S"] % 4, P * key_blocks(c["S"] % GROUPS)
                pool.wait_ge(r_done, turn.at(r_done, c["S"] + 1))
                part = probs[:, slot, :, 0:keys]
                nc.gpsimd.tensor_tensor(
                    part, part, inv_sum[:, slot].unsqueeze(2).broadcast_to([P, GROUP, keys]),
                    ALU.mult).then_inc(p_done, 1)
                c["S"] += 1

            def hidden_lo():
                slot = c["F"] % 2
                pool.wait_ge(h_hi, turn.at(h_hi, c["F"] + 1))
                pool.wait_ge(dn_done, turn.at(dn_done, c["F"] - 1))
                nc.gpsimd.tensor_tensor(
                    hid_lo[:, slot].rearrange("p c n -> p (c n)"), hid[:, slot],
                    hid_hi[:, slot].rearrange("p c n -> p (c n)").bitcast(F32),
                    ALU.subtract).then_inc(h_lo, 1)
                c["F"] += 1

            def body(second, first):
                if second:
                    powers()
                for t in range(NT):
                    for i in range(3):
                        rope_add(t, i)
                if second:
                    hidden_lo()
                    hidden_lo()
                if first:
                    powers()
                if second:
                    hidden_lo()
                normalise()
                for n in range(GROUPS):
                    if n + 1 < GROUPS:
                        normalise()
                    if n == 0 and second or first and 1 <= n <= PAIRS:
                        hidden_lo()
                    if first and n == 5:
                        powers()
                c["T"] += 6 + P_JOBS + second + 2 * first

            powers()
            for _ in range(PAIRS):
                hidden_lo()
            powers()
            c["T"] = 2
            body(0, 1)
            before = dict(c)
            with pool.Fori(1, BATCH - 1) as turn.now:
                body(1, 1)
            turn.now = None
            after_loop(c, before, per_turn, BATCH - 2)
            body(1, 0)
            powers()
            for _ in range(PAIRS):
                hidden_lo()

        @block.scalar
        def _(act):
            turn, per_turn = Turn(raised), dict(T=JOBS["T"], S=JOBS["S"], OT=JOBS["OT"], F=JOBS["F"], H=JOBS["F"],
                                         Y=JOBS["Y"], D=JOBS["D"])
            c = tally(**per_turn)

            def split_hi(i):
                act.wait_ge(w_in[i % 4], turn.at(w_in[i % 4], 16 * (i // 4 + 1)))
                _, dst, k = pieces[i]
                scale = 1.0
                if k is not None:
                    scale = gamma_sb[:, k:k + 1]
                    act.wait_ge(gamma_in, turn.at(gamma_in, 16))
                nc.scalar.activation(dst[0], stage(i), ACT.Copy, scale=scale).then_inc(w_hi, 1)

            def x_hi(dst, b):
                act.wait_ge(t_ready, turn.at(t_ready, c["T"] + 1))
                nc.scalar.activation(dst[0][:].rearrange("p k s -> p (k s)"), bank[b][:], ACT.Copy
                                     ).then_inc(t_hi, 1)
                c["T"] += 1

            def q_hi(t, i):
                act.wait_ge(t_ready, turn.at(t_ready, c["T"] + 1))
                src = bank[Q_T_BANK[t][i]][:].rearrange("p (a s) -> p a s", a=4)
                for odd in range(2):
                    rows = slice(DH * odd, DH * odd + DH)
                    last = nc.scalar.activation(q_t[rows, t, 8 * i + odd:8 * i + 8:2, :], src[rows], ACT.Copy)
                last.then_inc(t_hi, 1)
                c["T"] += 1

            def k_hi(t):
                act.wait_ge(t_ready, turn.at(t_ready, c["T"] + 1))
                nc.scalar.activation(k_t[0][:, :, t * P:t * P + P],
                                     bank[Q_T_BANK[t][2]][:].rearrange("p (h s) -> p h s", h=KV_HEADS), ACT.Copy
                                     ).then_inc(t_hi, 1)
                c["T"] += 1

            def p_hi(n):
                for kb in range(key_blocks(n)):
                    act.wait_ge(t_ready, turn.at(t_ready, c["T"] + 1))
                    nc.scalar.activation(p_t[0][:, kb], bank[p_bank(n, kb)][:], ACT.Copy
                                         ).then_inc(t_hi, 1)
                    c["T"] += 1

            def keep_x1():
                act.wait_ge(y_used, turn.at(y_used, c["Y"]))
                act.wait_ge(d_used, turn.at(d_used, c["D"]))
                nc.scalar.activation(x1[:], x1_next[:], ACT.Copy).then_inc(x1_kept, 1)

            def exps():
                slot, keys = c["S"] % 4, P * key_blocks(c["S"] % GROUPS)
                act.wait_ge(s_max, turn.at(s_max, c["S"] + 1))
                for g in range(GROUP):
                    part = probs[:, slot, g, 0:keys]
                    last = nc.scalar.activation(part, part, ACT.Exp, bias=neg_max[:, slot, g:g + 1],
                                                scale=DH ** -0.5, accum_out=row_sum[:, slot, g:g + 1])
                last.then_inc(e_done, 1)
                c["S"] += 1

            def o_split():
                act.wait_ge(o_ready, turn.at(o_ready, c["OT"] + 1))
                t, jp = c["OT"] // 2 % NT, c["OT"] % 2
                nc.scalar.activation(o_t[0][:, t, jp].rearrange("p g s -> p (g s)"), bank[O_BANK][:], ACT.Copy
                                     ).then_inc(o_hi, 1)
                c["OT"] += 1

            def tanh():
                slot = c["F"] % 2
                act.wait_ge(g_ready, turn.at(g_ready, c["F"] + 1))
                act.wait_ge(h_lo, turn.at(h_lo, c["F"] - 1))
                nc.scalar.activation(hid[:, slot], bank[G_BANK][:], ACT.Tanh, scale=0.5
                                     ).then_inc(th_done, 1)
                c["F"] += 1

            def hidden_hi():
                slot = c["H"] % 2
                act.wait_ge(mul_done, turn.at(mul_done, c["H"] + 1))
                act.wait_ge(dn_done, turn.at(dn_done, c["H"] - 1))
                nc.scalar.activation(hid_hi[:, slot].rearrange("p c n -> p (c n)"), hid[:, slot], ACT.Copy
                                     ).then_inc(h_hi, 1)
                c["H"] += 1

            def body(second, first):
                keep_x1()
                q_hi(0, 0), q_hi(0, 1), k_hi(0)
                if second:
                    x_hi(xf_t, F2_BANK)
                    tanh()
                q_hi(1, 0), q_hi(1, 1), k_hi(1)
                if second:
                    hidden_hi()
                    tanh()
                    hidden_hi()
                    tanh()
                    hidden_hi()
                exps()
                if second:
                    tanh()
                exps()
                if first:
                    x_hi(xf_t, F1_BANK)
                for n in range(GROUPS):
                    if n in (2, 4, 6):
                        o_split()
                    p_hi(n)
                    if n == 0 and second or first and 1 <= n <= PAIRS:
                        hidden_hi()
                    if n + 2 < GROUPS:
                        exps()
                    if first and n < PAIRS:
                        tanh()
                if first:
                    x_hi(xa_t, XA_BANK)
                o_split()
                c["Y"] += NT
                c["D"] += second + first

            for i in range(W_GATE_UP):
                split_hi(i)
            x_hi(xf_t, F1_BANK)
            for i in range(W_GATE_UP, W_DOWN):
                split_hi(i)
            for p in range(PAIRS):
                tanh()
                split_hi(W_DOWN + p)
                hidden_hi()
            for i in range(W_DOWN + PAIRS, W_ALL):
                split_hi(i)
            x_hi(xa_t, XA_BANK)
            c["D"] = 1
            body(0, 1)
            before = dict(c)
            with act.Fori(1, BATCH - 1) as turn.now:
                body(1, 1)
            turn.now = None
            after_loop(c, before, per_turn, BATCH - 2)
            body(1, 0)
            x_hi(xf_t, F2_BANK)
            for p in range(PAIRS):
                tanh()
                hidden_hi()

        @block.vector
        def _(dve):
            turn, per_turn = Turn(raised), dict(T=JOBS["T"], Q=JOBS["Q"], S=JOBS["S"], R=JOBS["S"], OT=JOBS["OT"],
                                         Y=JOBS["Y"], F=JOBS["F"], D=JOBS["D"], LN=JOBS["LN"], X=JOBS["X"],
                                         own=DVE_OWN)
            c = tally(**per_turn)

            def settle(instruction):
                instruction.then_inc(dve_own, 1)
                c["own"] += 1
                dve.wait_ge(dve_own, turn.at(dve_own, c["own"]))

            def split_lo(i):
                dve.wait_ge(w_hi, turn.at(w_hi, i + 1))
                _, dst, k = pieces[i]
                scale = 1.0 if k is None else gamma_sb[:, k:k + 1]
                nc.vector.scalar_tensor_tensor(out=dst[1], in0=stage(i), scalar=scale, in1=dst[0].bitcast(F32),
                                               op0=ALU.mult, op1=ALU.subtract).then_inc(w_lo, 1)

            def statistics(src):
                for t in range(NT):
                    last = nc.vector.bn_stats(stats[:, t], src[:, t])
                last.then_inc(dve_own, 1)
                c["own"] += 1
                value = turn.apart(dve, dve_own, c["own"])
                dve.wait_ge(eye_in, 16)
                dve.wait_ge(dve_own, value)
                for t in range(NT):
                    last = nc.vector.bn_aggr(mean_var[:, t], stats[:, t])
                settle(last)
                nc.vector.tensor_scalar(power_in[:, 0], mean_var[:, :, 1], EPS, None, ALU.add)
                nc.vector.tensor_copy(power_in[:, 1], mean_var[:, :, 1]).then_inc(ln_var, 1)

            def normal_rows(src, unit):
                dve.wait_ge(ln_pow, turn.at(ln_pow, c["LN"] + 1))
                dve.wait_ge(t_ready, turn.at(t_ready, c["T"]))
                rstd = power_out[:, 0]
                if unit:
                    settle(nc.vector.scalar_tensor_tensor(
                        out=factor[:], in0=power_out[:, 1], scalar=float(DIM) ** 0.5, in1=rstd,
                        op0=ALU.mult, op1=ALU.mult))
                    settle(nc.vector.tensor_scalar(factor[:], factor[:], NORM_MIN, None, ALU.max))
                    settle(nc.vector.reciprocal(factor[:], factor[:]))
                    settle(nc.vector.scalar_tensor_tensor(
                        out=factor[:], in0=factor[:], scalar=float(DIM) ** 0.5, in1=rstd,
                        op0=ALU.mult, op1=ALU.mult))
                    rstd = factor[:]
                for t in range(NT):
                    last = nc.vector.tensor_scalar(xn[:, t], src[:, t], mean_var[:, t, 0:1], rstd[:, t:t + 1],
                                                   ALU.subtract, ALU.mult)
                last.then_inc(xn_ready, 1)
                c["LN"] += 1

            def lo(dst, src, hi):
                dve.wait_ge(t_hi, turn.at(t_hi, c["T"] + 1))
                nc.vector.tensor_tensor(dst, src, hi.bitcast(F32), ALU.subtract).then_inc(t_lo, 1)
                c["T"] += 1

            def x_lo(dst, b):
                lo(dst[1][:].rearrange("p k s -> p (k s)"), bank[b][:], dst[0][:].rearrange("p k s -> p (k s)"))

            def q_lo(t, i):
                dve.wait_ge(t_hi, turn.at(t_hi, c["T"] + 1))
                src = bank[Q_T_BANK[t][i]][:].rearrange("p (a s) -> p a s", a=4)
                for odd in range(2):
                    rows, other = slice(DH * odd, DH * odd + DH), slice(DH - DH * odd, 2 * DH - DH * odd)
                    heads = slice(8 * i + odd, 8 * i + 8, 2)
                    last = nc.vector.tensor_tensor(q_t[other, t, heads, :], src[rows],
                                                   q_t[rows, t, heads, :].bitcast(F32), ALU.subtract)
                last.then_inc(t_lo, 1)
                c["T"] += 1

            def k_lo(t):
                lo(k_t[1][:, :, t * P:t * P + P],
                   bank[Q_T_BANK[t][2]][:].rearrange("p (h s) -> p h s", h=KV_HEADS),
                   k_t[0][:, :, t * P:t * P + P])

            def p_lo(n):
                for kb in range(key_blocks(n)):
                    lo(p_t[1][:, kb], bank[p_bank(n, kb)][:], p_t[0][:, kb])

            def rope_products(t, i):
                slot, b = c["Q"] % 2, bank[Q_BANKS[i]]
                heads, half = (8 if i < 2 else KV_HEADS), DH // 2
                src = b[:, 0:heads * DH].rearrange("p (h d) -> p h d", h=heads)
                dve.wait_ge(q_ready, turn.at(q_ready, c["Q"] + 1))
                dve.wait_ge(rope_sum, turn.at(rope_sum, c["Q"] - 1))
                nc.vector.tensor_tensor(rope_c[:, slot, 0:heads], src,
                                        rope_sb[:, t, 0].unsqueeze(1).broadcast_to([P, heads, DH]), ALU.mult)
                for s in range(2):
                    to, of = slice(half * s, half * s + half), slice(half - half * s, DH - half * s)
                    last = nc.vector.tensor_tensor(rope_s[:, slot, 0:heads, to], src[:, :, of],
                                                   rope_sb[:, t, 1, to].unsqueeze(1).broadcast_to([P, heads, half]),
                                                   ALU.mult)
                last.then_inc(rope_mul, 1)
                c["Q"] += 1
                if i == 2:
                    vals = b[:, KV_HEADS * DH:2 * KV_HEADS * DH].rearrange("p (a e d) -> p a e d", a=2, e=2)
                    pads = [v[:, t].rearrange("p a (e d) -> p a e d", e=3)[:, :, 0:3:2] for v in v_pad]
                    settle(nc.vector.tensor_copy(pads[0], vals))
                    nc.vector.tensor_tensor(pads[1], vals, pads[0].bitcast(F32), ALU.subtract
                                            ).then_inc(v_done, 1)

            def mask_max():
                slot, keys = c["S"] % 4, P * key_blocks(c["S"] % GROUPS)
                for g in range(GROUP):
                    if g % 2 == 0:
                        value = turn.apart(dve, s_ready, 2 * c["S"] + g // 2 + 1)
                        dve.wait_ge(eye_in, 16)
                        dve.wait_ge(s_ready, value)
                    last = nc.vector.tensor_tensor_reduce(
                        probs[:, slot, g, 0:keys], bank[S_BANKS[g // 2]][:, g % 2 * SEQ:g % 2 * SEQ + keys],
                        mask_sb[:, SEQ - keys:SEQ], 1.0, -3.4e38, ALU.add, ALU.max, row_max[:, slot, g:g + 1])
                    if g % 2:
                        last.then_inc(s_used, 1)
                dve.wait_ge(s_used, turn.at(s_used, 2 * c["S"] + 2))
                nc.vector.tensor_scalar(neg_max[:, slot], row_max[:, slot], -DH ** -0.5, None, ALU.mult
                                        ).then_inc(s_max, 1)
                c["S"] += 1

            def inverse():
                slot = c["R"] % 4
                dve.wait_ge(e_done, turn.at(e_done, c["R"] + 1))
                nc.vector.reciprocal(inv_sum[:, slot], row_sum[:, slot]).then_inc(r_done, 1)
                c["R"] += 1

            def o_split():
                dve.wait_ge(o_hi, turn.at(o_hi, c["OT"] + 1))
                t, jp = c["OT"] // 2 % NT, c["OT"] % 2
                nc.vector.tensor_tensor(
                    o_t[1][:, t, jp].rearrange("p g s -> p (g s)"), bank[O_BANK][:],
                    o_t[0][:, t, jp].rearrange("p g s -> p (g s)").bitcast(F32), ALU.subtract
                ).then_inc(o_lo, 1)
                c["OT"] += 1

            def attention_residual(t):
                dve.wait_ge(y_ready, turn.at(y_ready, c["Y"] + 1))
                dve.wait_ge(x1_kept, turn.at(x1_kept, c["X"]))
                dve.wait_ge(x_sent, turn.at(x_sent, 16 * (c["X"] - 1)))
                nc.vector.tensor_tensor(x2[:, t], bank[Y_BANKS[t]][:, 0:DIM], x1[:, t], ALU.add
                                        ).then_inc(y_used, 1)
                c["Y"] += 1

            def gate_up():
                slot = c["F"] % 2
                dve.wait_ge(th_done, turn.at(th_done, c["F"] + 1))
                nc.vector.scalar_tensor_tensor(out=hid[:, slot], in0=hid[:, slot], scalar=1.0, in1=bank[G_BANK][:],
                                               op0=ALU.add, op1=ALU.mult).then_inc(gate_used, 1)
                dve.wait_ge(u_ready, turn.at(u_ready, c["F"] + 1))
                dve.wait_ge(gate_used, turn.at(gate_used, c["F"] + 1))
                nc.vector.tensor_tensor(hid[:, slot], hid[:, slot], bank[U_BANK][:], ALU.mult
                                        ).then_inc(mul_done, 1)
                c["F"] += 1

            def ffn_residual(dst, src, kept=False):
                dve.wait_ge(dn_done, turn.at(dn_done, PAIRS * (c["D"] + 1)))
                if kept:
                    dve.wait_ge(x1_kept, turn.at(x1_kept, c["X"]))
                nc.vector.scalar_tensor_tensor(
                    out=dst[:].rearrange("p t d -> p (t d)"), in0=bank[D_BANK][:], scalar=0.25,
                    in1=src[:].rearrange("p t d -> p (t d)"), op0=ALU.mult, op1=ALU.add
                ).then_inc(d_used, 1)
                c["D"] += 1

            def body(second, first):
                c["X"] += 1
                if second:
                    dve.wait_ge(y_used, turn.at(y_used, c["Y"]))
                    statistics(x2)
                rope_products(0, 0), rope_products(0, 1)
                if second:
                    normal_rows(x2, False)
                rope_products(0, 2), rope_products(1, 0)
                q_lo(0, 0)
                rope_products(1, 1)
                q_lo(0, 1)
                rope_products(1, 2)
                k_lo(0)
                if second:
                    x_lo(xf_t, F2_BANK)
                    gate_up()
                q_lo(1, 0), q_lo(1, 1), k_lo(1)
                if second:
                    gate_up()
                    gate_up()
                if first:
                    dve.wait_ge(x_loaded, turn.at(x_loaded, 16 * (c["X"] + 1)))
                    statistics(x_in)
                mask_max()
                if first:
                    normal_rows(x_in, False)
                if second:
                    gate_up()
                inverse()
                mask_max()
                if first:
                    x_lo(xf_t, F1_BANK)
                for n in range(GROUPS):
                    if n in (2, 4, 6):
                        o_split()
                    p_lo(n)
                    if n + 1 < GROUPS:
                        inverse()
                    if n + 2 < GROUPS:
                        mask_max()
                    if n == 0 and second:
                        ffn_residual(x2, x2)
                    if first and n < PAIRS:
                        gate_up()
                    if first and n == 4:
                        ffn_residual(x1_next, x_in, True)
                    if first and n == 5:
                        dve.wait_ge(d_used, turn.at(d_used, c["D"]))
                        statistics(x1_next)
                    if first and n == 6:
                        normal_rows(x1_next, True)
                if first:
                    x_lo(xa_t, XA_BANK)
                attention_residual(0)
                o_split()
                attention_residual(1)

            dve.wait_ge(x_loaded, turn.at(x_loaded, 16))
            statistics(x_in)
            split_lo(0), split_lo(1)
            normal_rows(x_in, False)
            split_lo(2), split_lo(3)
            x_lo(xf_t, F1_BANK)
            split_lo(4), split_lo(5)
            for p in range(PAIRS):
                gate_up()
                split_lo(W_DOWN + p)
            for i in range(W_DOWN + PAIRS, W_ALL):
                split_lo(i)
            ffn_residual(x1_next, x_in)
            dve.wait_ge(d_used, turn.at(d_used, c["D"]))
            statistics(x1_next)
            normal_rows(x1_next, True)
            x_lo(xa_t, XA_BANK)
            dve.wait_ge(tables_in, turn.at(tables_in, 32))
            dve.wait_ge(pads_zero, turn.at(pads_zero, 2))
            body(0, 1)
            before = dict(c)
            with dve.Fori(1, BATCH - 1) as turn.now:
                body(1, 1)
            turn.now = None
            after_loop(c, before, per_turn, BATCH - 2)
            body(1, 0)
            dve.wait_ge(y_used, turn.at(y_used, c["Y"]))
            statistics(x2)
            normal_rows(x2, False)
            x_lo(xf_t, F2_BANK)
            for p in range(PAIRS):
                gate_up()
            ffn_residual(x2, x2)

        @block.tensor
        def _(pe):
            turn, per_turn = Turn(raised), dict(T=JOBS["T"], Q=JOBS["Q"], S=JOBS["S"], OT=JOBS["OT"], Y=JOBS["Y"],
                                        F=JOBS["F"], DN=JOBS["F"], D=JOBS["D"], LN=JOBS["LN"], V=NT,
                                        t2=JOBS["T"], t3=JOBS["T"], qk=JOBS["T"], ff=JOBS["T"])
            c = tally(**per_turn)

            def product(dst, a, b, start, stop, shared=False):
                for i, (x, y) in enumerate(((0, 0), (0, 1), (1, 0))):
                    last = nc.tensor.matmul(dst, a[x], b[y], start=start and i == 0, stop=stop and i == 2,
                                            skip_group_check=shared)
                return last

            def transposes(b, blocks):
                pe.wait_ge(t_lo, turn.at(t_lo, c["t2"] if b == T_BANKS[0] else c["t3"]))
                for i, block_in in enumerate(blocks):
                    last = nc.tensor.transpose(bank[b][:, i * P:i * P + P], block_in, eye_sb[:])
                last.then_inc(t_ready, 1)
                c["T"] += 1
                if b == T_BANKS[0]:
                    c["t2"] = c["T"]
                else:
                    c["t3"] = c["T"]

            def x_transposes(b):
                pe.wait_ge(xn_ready, turn.at(xn_ready, c["LN"] + 1))
                transposes(b, [xn[:, t, k * P:k * P + P] for k in range(KC) for t in range(NT)])
                c["LN"] += 1

            def ffn_transposes(b):
                x_transposes(b)
                c["ff"] = c["T"]

            def q_transposes(t, i):
                pe.wait_ge(rope_sum, turn.at(rope_sum, c["Q0"] + 3 * t + i + 1))
                if i < 2:
                    transposes(Q_T_BANK[t][i], [q_rot[:, i, a * P:a * P + P] for a in range(4)])
                else:
                    transposes(Q_T_BANK[t][i], [k_rot[:, j].rearrange("p c d -> p (c d)") for j in range(KV_HEADS)])
                    c["qk"] = c["T"]

            def qkv(t, i):
                if t == 0 and i == 0:
                    pe.wait_ge(t_lo, turn.at(t_lo, c["T"]))
                if t == 0 and i < 2:
                    pe.wait_ge(y_used, turn.at(y_used, c["Y"] - 1 + i))
                elif t == 1 and i < 2:
                    pe.wait_ge(rope_mul, turn.at(rope_mul, c["Q"] - 2))
                elif t == 1:
                    pe.wait_ge(v_done, turn.at(v_done, c["V"] + 1))
                rows = slice(t * P, t * P + P)
                for k in range(KC):
                    last = product(bank[Q_BANKS[i]][:], [x[:, k, rows] for x in xa_t],
                                   [w[:, k, 512 * i:512 * i + 512] for w in qkv_w], k == 0, k == KC - 1)
                last.then_inc(q_ready, 1)
                c["Q"] += 1

            def scores():
                n = c["S"] % GROUPS
                t, j = n // KV_HEADS, n % KV_HEADS
                pe.wait_ge(t_lo, turn.at(t_lo, c["qk"]))
                for g in range(GROUP):
                    if g % 2 == 0:
                        pe.wait_ge(s_used, turn.at(s_used, 2 * c["S"] - 1 + g // 2))
                    dst = bank[S_BANKS[g // 2]][:, g % 2 * SEQ:g % 2 * SEQ + SEQ]
                    for s in range(2):
                        last = nc.tensor.matmul(dst, q_t[:, t, KV_HEADS * g + j, :], k_t[s][:, j, :],
                                                start=s == 0, stop=s == 1)
                    if g % 2:
                        last.then_inc(s_ready, 1)
                c["S"] += 1

            def p_transposes(n):
                pe.wait_ge(p_done, turn.at(p_done, c["P0"] + n + 1))
                for kb in range(key_blocks(n)):
                    transposes(p_bank(n, kb), [probs[:, n % 4, g, kb * P:kb * P + P] for g in range(GROUP)])
                c["p"] = c["T"]

            def values(n):
                t, j = n // KV_HEADS, n % KV_HEADS
                odd = j % 2 == 1
                pe.wait_ge(t_lo, turn.at(t_lo, c["p"]))
                if n % KV_HEADS == 0:
                    pe.wait_ge(v_done, turn.at(v_done, c["V"]))
                if not odd:
                    pe.wait_ge(o_lo, turn.at(o_lo, c["OT"]))
                for kb in range(t + 1):
                    last = product(bank[O_BANK][:], [v[:, kb, j // 2, DH * odd:DH * odd + P] for v in v_pad],
                                   [x[:, kb] for x in p_t], not odd and kb == 0, odd and kb == t)
                if odd:
                    last.then_inc(o_ready, 1)
                    c["OT"] += 1

            def projection(t):
                pe.wait_ge(o_lo, turn.at(o_lo, c["OT"]))
                pe.wait_ge(s_used, turn.at(s_used, 2 * c["S"]))
                for k in range(OC):
                    last = product(bank[Y_BANKS[t]][:, 0:DIM], [o[:, t, k % 2, k // 2] for o in o_t],
                                   [w[:, k] for w in out_w], k == 0, k == OC - 1)
                last.then_inc(y_ready, 1)
                c["Y"] += 1

            def gate_and_up():
                p = c["F"] % PAIRS
                pe.wait_ge(t_lo, turn.at(t_lo, c["ff"]))
                for weight, b, used, ready in ((gate_w, G_BANK, gate_used, g_ready), (up_w, U_BANK, mul_done, u_ready)):
                    pe.wait_ge(used, turn.at(used, c["F"]))
                    for h in range(2):
                        cols = slice((2 * p + h) * P, (2 * p + h + 1) * P)
                        for k in range(KC):
                            last = product(bank[b][:, h * SEQ:h * SEQ + SEQ], [w[:, k, cols] for w in weight],
                                           [x[:, k] for x in xf_t], k == 0, k == KC - 1)
                    last.then_inc(ready, 1)
                c["F"] += 1

            def down():
                p, slot = c["DN"] % PAIRS, c["DN"] % 2
                pe.wait_ge(h_lo, turn.at(h_lo, c["DN"] + 1))
                if p == 0:
                    pe.wait_ge(d_used, turn.at(d_used, c["D"]))
                for t in range(NT):
                    for h in range(2):
                        last = product(bank[D_BANK][:, t * DIM:t * DIM + DIM],
                                       [x[:, slot, h, t * P:t * P + P] for x in (hid_hi, hid_lo)],
                                       [w[:, 2 * p + h] for w in down_w],
                                       p == 0 and t == 0 and h == 0, p == PAIRS - 1 and t == NT - 1 and h == 1,
                                       shared=True)
                last.then_inc(dn_done, 1)
                c["DN"] += 1
                if p == PAIRS - 1:
                    c["D"] += 1

            def body(second, first):
                c["P0"], c["Q0"] = c["S"], c["Q"]
                qkv(0, 0), qkv(0, 1), qkv(0, 2), qkv(1, 0)
                q_transposes(0, 0)
                qkv(1, 1)
                q_transposes(0, 1)
                qkv(1, 2)
                c["V"] += NT
                q_transposes(0, 2)
                if second:
                    ffn_transposes(F2_BANK)
                    gate_and_up()
                q_transposes(1, 0), q_transposes(1, 1), q_transposes(1, 2)
                if second:
                    gate_and_up()
                    down()
                    gate_and_up()
                    down()
                scores()
                if second:
                    gate_and_up()
                    down()
                scores()
                if first:
                    ffn_transposes(F1_BANK)
                for n in range(GROUPS):
                    if n:
                        values(n - 1)
                    p_transposes(n)
                    if n + 2 < GROUPS:
                        scores()
                    if n == 0 and second:
                        down()
                    if first and n < PAIRS:
                        gate_and_up()
                    if first and 1 <= n <= PAIRS:
                        down()
                if first:
                    x_transposes(XA_BANK)
                projection(0)
                values(GROUPS - 1)
                projection(1)

            pe.wait_ge(eye_in, turn.at(eye_in, 16))
            ffn_transposes(F1_BANK)
            pe.wait_ge(w_lo, turn.at(w_lo, W_GATE_UP))
            gate_and_up()
            gate_and_up()
            pe.wait_ge(w_lo, turn.at(w_lo, W_DOWN))
            down()
            gate_and_up()
            down()
            gate_and_up()
            down()
            down()
            x_transposes(XA_BANK)
            pe.wait_ge(w_lo, turn.at(w_lo, W_ALL))
            body(0, 1)
            before = dict(c)
            with pe.Fori(1, BATCH - 1) as turn.now:
                body(1, 1)
            turn.now = None
            after_loop(c, before, per_turn, BATCH - 2)
            body(1, 0)
            ffn_transposes(F2_BANK)
            gate_and_up()
            for _ in range(PAIRS - 1):
                gate_and_up()
                down()
            down()


_INS = ["x", "w_gate", "w_up", "w_down", "w_qkv", "w_out", "gamma", "rope", "mask", "eye"]


def _chunks(w):
    return np.ascontiguousarray(w.reshape(w.shape[0] // P, P, w.shape[1]).transpose(1, 0, 2))


def _rope_table():
    inv = np.float32(10000.0) ** -(np.arange(0, DH, 2, dtype=np.float32) / np.float32(DH))
    angle = (np.arange(SEQ, dtype=np.float32)[:, None] * inv[None, :].astype(np.float32)).astype(np.float64)
    cos, sin = np.cos(angle), np.sin(angle)
    table = np.stack([np.concatenate([cos, cos], 1), np.concatenate([-sin, sin], 1)], 1)
    return np.ascontiguousarray(table.reshape(NT, P, 2, DH).transpose(1, 0, 2, 3).astype(np.float32))


def kernel(L0_attn_x, L0_attn_gamma, L0_attn_w_qkv, L0_attn_w_out, L0_ffn_w_gate, L0_ffn_w_up, L0_ffn_w_down):
    import concourse.bacc as _bacc
    from concourse.bass_utils import run_bass_kernel_spmd as _run

    causal = np.where(np.tril(np.ones((P, P), bool)), 0.0, MASKED).astype(np.float32)
    given = {
        "x": np.ascontiguousarray(L0_attn_x),
        "w_gate": _chunks(np.asarray(L0_ffn_w_gate).T),
        "w_up": _chunks(np.asarray(L0_ffn_w_up).T),
        "w_down": _chunks(np.asarray(L0_ffn_w_down).T),
        "w_qkv": _chunks(np.asarray(L0_attn_w_qkv)),
        "w_out": _chunks(np.asarray(L0_attn_w_out)),
        "gamma": np.ascontiguousarray(np.asarray(L0_attn_gamma).reshape(KC, P).T),
        "rope": _rope_table(),
        "mask": np.concatenate([np.zeros((P, SEQ - P), np.float32), causal], 1),
        "eye": np.eye(P, dtype=np.float32),
    }
    nc = _bacc.Bacc("TRN2", target_bir_lowering=False, num_devices=1)
    args = [nc.dram_tensor(f"in_{n}", given[n].shape, F32, kind="ExternalInput").ap() for n in _INS]
    out = nc.dram_tensor("out_0", (BATCH, SEQ, DIM), F32, kind="ExternalOutput").ap()
    build(nc, *args, out)
    r = _run(nc, [{f"in_{n}": given[n] for n in _INS}], core_ids=[0])
    return r.results[0]["out_0"]
```

```python
import numpy as np
import concourse.bass as bass
from concourse import mybir
from contextlib import ExitStack

F32 = mybir.dt.float32
F32R = mybir.dt.float32r
ALU = mybir.AluOpType
ACT = mybir.ActivationFunctionType

BATCH, SEQ, DIM = 8, 256, 256
HEADS, KV_HEADS, DH = 16, 4, 64
GROUP = HEADS // KV_HEADS
HID = 1024
P = 128
NT = SEQ // P
KC = DIM // P
QKV = (HEADS + 2 * KV_HEADS) * DH
PAIRS = HID // (2 * P)
OC = HEADS * DH // P
MASKED = -3.0e38
EPS = 1e-5
NORM_MIN = 1e-12
GROUPS = NT * KV_HEADS


def key_blocks(n):
    return n // KV_HEADS + 1


def transpose_jobs(second, first):
    return (["first"] * first + [("q", t, i) for t in range(NT) for i in range(3)] + ["second"] * second
            + [("p", n, kb) for n in range(GROUPS) for kb in range(key_blocks(n))] + ["attention"] * first)


class Turn:

    def __init__(self, per_turn):
        self.per_turn, self.now = per_turn, None

    def at(self, semaphore, count):
        if self.now is None:
            return max(count, 0)
        per_turn = self.per_turn[semaphore.name]
        assert count > 0 and per_turn
        return (self.now - 1) * per_turn + count

    def apart(self, engine, semaphore, count):
        value = self.at(semaphore, count)
        return value if self.now is None else engine.to_reg(value)


def tally(**kinds):
    return {kind: 0 for kind in kinds}


def after_loop(c, before, per_turn, turns):
    for kind, n in per_turn.items():
        assert c[kind] - before[kind] == n, (kind, c[kind] - before[kind])
        c[kind] += (turns - 1) * n


JOBS = dict(T=len(transpose_jobs(1, 1)), Q=6, S=GROUPS, V=GROUPS, OT=GROUPS // 2, Y=NT, F=2 * PAIRS, D=2, LN=3, X=1, W=1)


def build(nc, x, w_gate, w_up, w_down, w_qkv, w_out, gamma, rope, mask, eye, out):
    ctx = ExitStack()
    with ctx:
        def sb(name, shape, dt=F32):
            return ctx.enter_context(nc.sbuf_tensor(name, shape, dt))

        raised = {}

        def sig(name, per_turn=0):
            semaphore = ctx.enter_context(nc.semaphore(name))
            raised[semaphore.name] = per_turn
            return semaphore

        gate_w = [sb(f"gate_{s}", [P, KC, HID], F32R) for s in ("hi", "lo")]
        up_w = [sb(f"up_{s}", [P, KC, HID], F32R) for s in ("hi", "lo")]
        down_w = [sb(f"down_{s}", [P, HID // P, DIM], F32R) for s in ("hi", "lo")]
        qkv_w = [sb(f"qkv_{s}", [P, KC, QKV], F32R) for s in ("hi", "lo")]
        out_w = [sb(f"out_{s}", [P, OC, DIM], F32R) for s in ("hi", "lo")]
        gamma_sb = sb("gamma_sb", [P, KC])
        rope_sb = sb("rope_sb", [P, NT, 2, DH])
        mask_sb = sb("mask_sb", [P, SEQ])
        eye_sb = sb("eye_sb", [P, P])
        exponent = sb("exponent", [P, 2, NT])

        x_in = sb("x_in", [P, NT, DIM])
        x1_next = sb("x1_next", [P, NT, DIM])
        x1 = sb("x1", [P, NT, DIM])
        x2 = sb("x2", [P, NT, DIM])
        y_out = sb("y_out", [P, NT, DIM])
        xn = sb("xn", [P, NT, DIM])
        xf_t = [sb(f"xf_t_{s}", [P, KC, SEQ], F32R) for s in ("hi", "lo")]
        xa_t = [sb(f"xa_t_{s}", [P, KC, SEQ], F32R) for s in ("hi", "lo")]
        stats = sb("stats", [P, NT, 6])
        mean_var = sb("mean_var", [P, NT, 2])
        power_in = sb("power_in", [P, 2, NT])
        power_out = sb("power_out", [P, 2, NT])
        factor = sb("factor", [P, NT])

        hid = sb("hid", [P, 2, 2 * P * NT])
        hid_hi = sb("hid_hi", [P, 2, 2, SEQ], F32R)
        hid_lo = sb("hid_lo", [P, 2, 2, SEQ], F32R)

        rope_c = sb("rope_c", [P, 2, 8, DH])
        rope_s = sb("rope_s", [P, 2, 8, DH])
        q_rot = sb("q_rot", [P, 2, 8 * DH])
        k_rot = sb("k_rot", [P, KV_HEADS, 2, DH])
        q_t = sb("q_t", [P, NT, HEADS, P], F32R)
        k_t = [sb(f"k_t_{s}", [P, KV_HEADS, SEQ], F32R) for s in ("hi", "lo")]
        v_halves = sb("v_halves", [P, NT, KV_HEADS, 2 * DH], F32R)
        probs = sb("probs", [P, 4, GROUP, SEQ])
        row_max = sb("row_max", [P, 4, GROUP])
        neg_max = sb("neg_max", [P, 4, GROUP])
        row_sum = sb("row_sum", [P, 4, GROUP])
        inv_sum = sb("inv_sum", [P, 4, GROUP])
        p_t = [sb(f"p_t_{s}", [P, NT, GROUP * P], F32R) for s in ("hi", "lo")]
        o_sums = sb("o_sums", [P, GROUP * P])
        o_t = [sb(f"o_t_{s}", [P, NT, 2, GROUP, P], F32R) for s in ("hi", "lo")]

        bank = [ctx.enter_context(nc.psum_tensor(f"bank{i}", [P, 512], F32)) for i in range(8)]
        Q_BANKS, S_BANKS, Y_BANKS, T_BANKS = (0, 1, 4), (0, 1), (0, 1), (2, 3)
        O_BANK, G_BANK, U_BANK, D_BANK = 4, 5, 6, 7
        T_BANK = {job: T_BANKS[i % 2] for i, job in enumerate(transpose_jobs(1, 1))}

        eye_in, gamma_in, rope_in = sig("eye_in"), sig("gamma_in"), sig("rope_in")
        w_in = [sig(f"w_in{i}") for i in range(4)]
        w_hi, w_lo = sig("w_hi"), sig("w_lo")
        exponents_set = sig("exponents_set")
        x_loaded = sig("x_loaded", 16)
        x_sent = sig("x_sent", 16)
        x1_kept = sig("x1_kept", 1)
        ln_var = sig("ln_var", JOBS["LN"])
        ln_pow = sig("ln_pow", JOBS["LN"])
        xn_ready = sig("xn_ready", JOBS["LN"])
        t_ready, t_hi, t_lo = (sig(n, JOBS["T"]) for n in ("t_ready", "t_hi", "t_lo"))
        q_ready = sig("q_ready", 6)
        rope_mul, rope_sum = sig("rope_mul", 6), sig("rope_sum", 6)
        v_done = sig("v_done", NT)
        s_ready, s_used = sig("s_ready", 2 * GROUPS), sig("s_used", 2 * GROUPS)
        s_max, e_done, r_done, p_done = (sig(n, GROUPS) for n in ("s_max", "e_done", "r_done", "p_done"))
        o_ready, o_small, o_sum = (sig(n, JOBS["V"]) for n in ("o_ready", "o_small", "o_sum"))
        o_hi, o_lo = (sig(n, JOBS["OT"]) for n in ("o_hi", "o_lo"))
        y_ready, y_used = sig("y_ready", NT), sig("y_used", NT)
        g_ready, u_ready, th_done, gate_used, mul_done, h_hi, h_lo, dn_done = (
            sig(n, JOBS["F"]) for n in
            ("g_ready", "u_ready", "th_done", "gate_used", "mul_done", "h_hi", "h_lo", "dn_done"))
        d_used = sig("d_used", JOBS["D"])
        DVE_OWN = 3 * 2 + 4 + NT
        dve_own = sig("dve_own", DVE_OWN)

        pieces = []
        for w, dst, name in ((w_gate, gate_w, "gate"), (w_up, up_w, "up")):
            pieces += [(w[:, k, :], [d[:, k, :] for d in dst], None) for k in range(KC)]
        half = HID // P // 2
        pieces += [(w_down[:, half * i:half * i + half, :].rearrange("p c n -> p (c n)"),
                    [d[:, half * i:half * i + half, :].rearrange("p c n -> p (c n)") for d in down_w], None)
                   for i in range(2)]
        pieces += [(w_qkv[:, k, i:i + QKV // 2], [d[:, k, i:i + QKV // 2] for d in qkv_w], k)
                   for k in range(KC) for i in (0, QKV // 2)]
        pieces += [(w_out[:, half * i:half * i + half, :].rearrange("p c n -> p (c n)"),
                    [d[:, half * i:half * i + half, :].rearrange("p c n -> p (c n)") for d in out_w], None)
                   for i in range(2)]
        W_GATE_UP, W_DOWN, W_ALL = 2 * KC, 2 * KC + 2, len(pieces)

        def stage(i):
            n = pieces[i][0].shape[1]
            return probs[:, i % 4].rearrange("p g k -> p (g k)")[:, 0:n]

        block = ctx.enter_context(nc.Block())

        @block.sync
        def _(sp):
            turn = Turn(raised)

            def load_x(m):
                sp.dma_start(x_in[:], x[bass.ds(m, 1)].rearrange("o (t p) d -> p (o t) d", p=P)
                             ).then_inc(x_loaded, 16)

            def store(m):
                sp.dma_start(out[bass.ds(m, 1)].rearrange("o (t p) d -> p (o t) d", p=P), y_out[:]
                             ).then_inc(x_sent, 16)

            load_x(0)
            sp.dma_start(eye_sb[:], eye).then_inc(eye_in, 16)
            sp.dma_start(gamma_sb[:], gamma).then_inc(gamma_in, 16)
            for i, (src, _, _) in enumerate(pieces):
                if i >= 4:
                    sp.wait_ge(w_lo, turn.at(w_lo, i - 3))
                sp.dma_start(stage(i), src).then_inc(w_in[i % 4], 16)
                if i == W_GATE_UP:
                    sp.dma_start(rope_sb[:], rope).then_inc(rope_in, 16)
                    sp.dma_start(mask_sb[:], mask).then_inc(x_sent, 16)
            for m in (1, 2):
                sp.wait_ge(d_used, turn.at(d_used, m))
                load_x(m)
            with sp.Fori(1, BATCH - 2) as turn.now:
                sp.wait_ge(d_used, turn.at(d_used, 3))
                load_x(turn.now + 2)
                sp.wait_ge(d_used, turn.at(d_used, 4))
                store(turn.now - 1)
            turn.now = None
            used = 2 + 2 * (BATCH - 3)
            for m, more in ((BATCH - 3, 2), (BATCH - 2, 3), (BATCH - 1, 4)):
                sp.wait_ge(d_used, turn.at(d_used, used + more))
                store(m)
            sp.wait_ge(x_sent, turn.at(x_sent, 16 + 16 * BATCH))

        @block.gpsimd
        def _(pool):
            turn, per_turn = Turn(raised), dict(T=JOBS["T"], Q=JOBS["Q"], S=JOBS["S"], F=JOBS["F"], LN=JOBS["LN"],
                                         OT=JOBS["OT"])
            c = tally(**per_turn)
            nc.gpsimd.memset(exponent[:, 0], -0.5).then_inc(exponents_set, 1)
            nc.gpsimd.memset(exponent[:, 1], 0.5).then_inc(exponents_set, 1)
            pool.wait_ge(exponents_set, turn.at(exponents_set, 2))

            def powers():
                pool.wait_ge(ln_var, turn.at(ln_var, c["LN"] + 1))
                nc.gpsimd.tensor_tensor(power_out[:], power_in[:], exponent[:], ALU.pow
                                        ).then_inc(ln_pow, 1)
                c["LN"] += 1

            def rope_add(jobs, t, i):
                slot = c["Q"] % 2
                pool.wait_ge(rope_mul, turn.at(rope_mul, c["Q"] + 1))
                pool.wait_ge(t_ready, turn.at(t_ready, c["T"] + (jobs.index(("q", 0, i)) + 1 if t else 0)))
                if i < 2:
                    nc.gpsimd.tensor_tensor(
                        q_rot[:, i], rope_c[:, slot].rearrange("p h d -> p (h d)"),
                        rope_s[:, slot].rearrange("p h d -> p (h d)"), ALU.add).then_inc(rope_sum, 1)
                else:
                    for copy in range(2):
                        last = nc.gpsimd.tensor_tensor(
                            k_rot[:, :, copy, :], rope_c[:, slot, 0:KV_HEADS],
                            rope_s[:, slot, 0:KV_HEADS], ALU.add)
                    last.then_inc(rope_sum, 1)
                c["Q"] += 1

            def normalise():
                slot, keys = c["S"] % 4, P * key_blocks(c["S"] % GROUPS)
                pool.wait_ge(r_done, turn.at(r_done, c["S"] + 1))
                part = probs[:, slot, :, 0:keys]
                nc.gpsimd.tensor_tensor(
                    part, part, inv_sum[:, slot].unsqueeze(2).broadcast_to([P, GROUP, keys]),
                    ALU.mult).then_inc(p_done, 1)
                c["S"] += 1

            def hidden_lo():
                slot = c["F"] % 2
                pool.wait_ge(h_hi, turn.at(h_hi, c["F"] + 1))
                pool.wait_ge(dn_done, turn.at(dn_done, c["F"] - 1))
                nc.gpsimd.tensor_tensor(
                    hid_lo[:, slot].rearrange("p c n -> p (c n)"), hid[:, slot],
                    hid_hi[:, slot].rearrange("p c n -> p (c n)").bitcast(F32),
                    ALU.subtract).then_inc(h_lo, 1)
                c["F"] += 1

            def outputs_lo():
                t, jp = c["OT"] // 2 % NT, c["OT"] % 2
                pool.wait_ge(o_hi, turn.at(o_hi, c["OT"] + 1))
                nc.gpsimd.tensor_tensor(
                    o_t[1][:, t, jp].rearrange("p g s -> p (g s)"), o_sums[:],
                    o_t[0][:, t, jp].rearrange("p g s -> p (g s)").bitcast(F32), ALU.subtract
                ).then_inc(o_lo, 1)
                c["OT"] += 1

            def body(second, first):
                jobs = transpose_jobs(second, first)
                if first:
                    powers()
                rope_add(jobs, 0, 0), rope_add(jobs, 0, 1), rope_add(jobs, 0, 2), rope_add(jobs, 1, 0)
                rope_add(jobs, 1, 1), rope_add(jobs, 1, 2)
                if first:
                    hidden_lo(), hidden_lo()
                if second:
                    powers()
                normalise()
                if first:
                    hidden_lo()
                normalise(), normalise(), normalise(), outputs_lo()
                if first:
                    hidden_lo()
                normalise(), normalise(), outputs_lo()
                if second:
                    hidden_lo()
                normalise()
                if second:
                    hidden_lo()
                normalise(), outputs_lo()
                if second:
                    hidden_lo()
                if first:
                    powers()
                if second:
                    hidden_lo()
                outputs_lo()
                c["T"] += len(jobs)

            powers()
            for _ in range(PAIRS):
                hidden_lo()
            powers()
            c["T"] = 2
            body(0, 1)
            before = dict(c)
            with pool.Fori(1, BATCH - 1) as turn.now:
                body(1, 1)
            turn.now = None
            after_loop(c, before, per_turn, BATCH - 2)
            body(1, 0)
            powers()
            for _ in range(PAIRS):
                hidden_lo()

        @block.scalar
        def _(act):
            turn, per_turn = Turn(raised), dict(T=JOBS["T"], S=JOBS["S"], V=JOBS["V"], OT=JOBS["OT"], F=JOBS["F"], H=JOBS["F"],
                                         Y=JOBS["Y"], D=JOBS["D"])
            c = tally(**per_turn)

            def split_hi(i):
                act.wait_ge(w_in[i % 4], turn.at(w_in[i % 4], 16 * (i // 4 + 1)))
                _, dst, k = pieces[i]
                scale = 1.0
                if k is not None:
                    scale = gamma_sb[:, k:k + 1]
                    act.wait_ge(gamma_in, turn.at(gamma_in, 16))
                nc.scalar.activation(dst[0], stage(i), ACT.Copy, scale=scale).then_inc(w_hi, 1)

            def x_hi(dst, job):
                act.wait_ge(t_ready, turn.at(t_ready, c["T"] + 1))
                nc.scalar.activation(dst[0][:].rearrange("p k s -> p (k s)"), bank[T_BANK[job]][:], ACT.Copy
                                     ).then_inc(t_hi, 1)
                c["T"] += 1

            def q_hi(t, i):
                act.wait_ge(t_ready, turn.at(t_ready, c["T"] + 1))
                src = bank[T_BANK["q", t, i]][:].rearrange("p (a s) -> p a s", a=4)
                for odd in range(2):
                    rows = slice(DH * odd, DH * odd + DH)
                    last = nc.scalar.activation(q_t[rows, t, 8 * i + odd:8 * i + 8:2, :], src[rows], ACT.Copy)
                last.then_inc(t_hi, 1)
                c["T"] += 1

            def k_hi(t):
                act.wait_ge(t_ready, turn.at(t_ready, c["T"] + 1))
                nc.scalar.activation(k_t[0][:, :, t * P:t * P + P],
                                     bank[T_BANK["q", t, 2]][:].rearrange("p (h s) -> p h s", h=KV_HEADS), ACT.Copy
                                     ).then_inc(t_hi, 1)
                c["T"] += 1

            def p_hi(n):
                for kb in range(key_blocks(n)):
                    act.wait_ge(t_ready, turn.at(t_ready, c["T"] + 1))
                    nc.scalar.activation(p_t[0][:, kb], bank[T_BANK["p", n, kb]][:], ACT.Copy
                                         ).then_inc(t_hi, 1)
                    c["T"] += 1

            def keep_x1():
                act.wait_ge(y_used, turn.at(y_used, c["Y"]))
                act.wait_ge(d_used, turn.at(d_used, c["D"]))
                nc.scalar.activation(x1[:], x1_next[:], ACT.Copy).then_inc(x1_kept, 1)

            def exps():
                slot, keys = c["S"] % 4, P * key_blocks(c["S"] % GROUPS)
                act.wait_ge(s_max, turn.at(s_max, c["S"] + 1))
                for g in range(GROUP):
                    part = probs[:, slot, g, 0:keys]
                    last = nc.scalar.activation(part, part, ACT.Exp, bias=neg_max[:, slot, g:g + 1],
                                                scale=DH ** -0.5, accum_out=row_sum[:, slot, g:g + 1])
                last.then_inc(e_done, 1)
                c["S"] += 1

            def small_half(n):
                odd = n % 2
                act.wait_ge(o_ready, turn.at(o_ready, c["V"] + 1))
                if not odd:
                    act.wait_ge(o_lo, turn.at(o_lo, c["OT"]))
                rows, other = slice(DH * odd, DH * odd + DH), slice(DH - DH * odd, 2 * DH - DH * odd)
                nc.scalar.activation(o_sums[rows], bank[O_BANK][other], ACT.Copy).then_inc(o_small, 1)
                c["V"] += 1

            def outputs_hi():
                t, jp = c["OT"] // 2 % NT, c["OT"] % 2
                act.wait_ge(o_sum, turn.at(o_sum, 2 * c["OT"] + 2))
                nc.scalar.activation(o_t[0][:, t, jp].rearrange("p g s -> p (g s)"), o_sums[:], ACT.Copy
                                     ).then_inc(o_hi, 1)
                c["OT"] += 1

            def tanh():
                slot = c["F"] % 2
                act.wait_ge(g_ready, turn.at(g_ready, c["F"] + 1))
                act.wait_ge(h_lo, turn.at(h_lo, c["F"] - 1))
                nc.scalar.activation(hid[:, slot], bank[G_BANK][:], ACT.Tanh, scale=0.5
                                     ).then_inc(th_done, 1)
                c["F"] += 1

            def hidden_hi():
                slot = c["H"] % 2
                act.wait_ge(mul_done, turn.at(mul_done, c["H"] + 1))
                act.wait_ge(dn_done, turn.at(dn_done, c["H"] - 1))
                nc.scalar.activation(hid_hi[:, slot].rearrange("p c n -> p (c n)"), hid[:, slot], ACT.Copy
                                     ).then_inc(h_hi, 1)
                c["H"] += 1

            def body(second, first):
                if first:
                    x_hi(xf_t, "first")
                q_hi(0, 0), q_hi(0, 1)
                if first:
                    tanh()
                keep_x1(), k_hi(0)
                if first:
                    hidden_hi(), tanh()
                q_hi(1, 0), q_hi(1, 1), k_hi(1)
                if first:
                    tanh(), hidden_hi()
                exps()
                if first:
                    tanh(), hidden_hi()
                exps()
                if second:
                    x_hi(xf_t, "second")
                p_hi(0), exps(), small_half(0), p_hi(1), exps()
                if first:
                    hidden_hi()
                if second:
                    tanh()
                small_half(1), p_hi(2), outputs_hi(), exps(), p_hi(3), small_half(2)
                if second:
                    tanh()
                exps(), small_half(3), p_hi(4)
                if second:
                    hidden_hi()
                outputs_hi(), exps(), small_half(4), p_hi(5)
                if second:
                    hidden_hi(), tanh()
                exps(), small_half(5), p_hi(6)
                if second:
                    hidden_hi()
                outputs_hi()
                if second:
                    tanh()
                small_half(6), p_hi(7)
                if second:
                    hidden_hi()
                small_half(7), outputs_hi()
                if first:
                    x_hi(xa_t, "attention")
                c["Y"] += NT
                c["D"] += second + first

            for i in range(W_GATE_UP):
                split_hi(i)
            x_hi(xf_t, "first")
            for i in range(W_GATE_UP, W_DOWN):
                split_hi(i)
            for p in range(PAIRS):
                tanh()
                split_hi(W_DOWN + p)
                hidden_hi()
            for i in range(W_DOWN + PAIRS, W_ALL):
                split_hi(i)
            x_hi(xa_t, "attention")
            c["D"] = 1
            body(0, 1)
            before = dict(c)
            with act.Fori(1, BATCH - 1) as turn.now:
                body(1, 1)
            turn.now = None
            after_loop(c, before, per_turn, BATCH - 2)
            body(1, 0)
            x_hi(xf_t, "second")
            for p in range(PAIRS):
                tanh()
                hidden_hi()

        @block.vector
        def _(dve):
            turn, per_turn = Turn(raised), dict(T=JOBS["T"], Q=JOBS["Q"], S=JOBS["S"], R=JOBS["S"], V=JOBS["V"],
                                         Y=JOBS["Y"], F=JOBS["F"], D=JOBS["D"], LN=JOBS["LN"], X=JOBS["X"], W=1,
                                         own=DVE_OWN)
            c = tally(**per_turn)

            def settle(instruction):
                instruction.then_inc(dve_own, 1)
                c["own"] += 1
                dve.wait_ge(dve_own, turn.at(dve_own, c["own"]))

            def split_lo(i):
                dve.wait_ge(w_hi, turn.at(w_hi, i + 1))
                _, dst, k = pieces[i]
                scale = 1.0 if k is None else gamma_sb[:, k:k + 1]
                nc.vector.scalar_tensor_tensor(out=dst[1], in0=stage(i), scalar=scale, in1=dst[0].bitcast(F32),
                                               op0=ALU.mult, op1=ALU.subtract).then_inc(w_lo, 1)

            def statistics(src):
                for t in range(NT):
                    last = nc.vector.bn_stats(stats[:, t], src[:, t])
                last.then_inc(dve_own, 1)
                c["own"] += 1
                value = turn.apart(dve, dve_own, c["own"])
                dve.wait_ge(eye_in, 16)
                dve.wait_ge(dve_own, value)
                for t in range(NT):
                    last = nc.vector.bn_aggr(mean_var[:, t], stats[:, t])
                settle(last)
                nc.vector.tensor_scalar(power_in[:, 0], mean_var[:, :, 1], EPS, None, ALU.add)
                nc.vector.tensor_copy(power_in[:, 1], mean_var[:, :, 1]).then_inc(ln_var, 1)

            def normal_rows(src, unit):
                dve.wait_ge(ln_pow, turn.at(ln_pow, c["LN"] + 1))
                dve.wait_ge(t_ready, turn.at(t_ready, c["T"]))
                rstd = power_out[:, 0]
                if unit:
                    settle(nc.vector.scalar_tensor_tensor(
                        out=factor[:], in0=power_out[:, 1], scalar=float(DIM) ** 0.5, in1=rstd,
                        op0=ALU.mult, op1=ALU.mult))
                    settle(nc.vector.tensor_scalar(factor[:], factor[:], NORM_MIN, None, ALU.max))
                    settle(nc.vector.reciprocal(factor[:], factor[:]))
                    settle(nc.vector.scalar_tensor_tensor(
                        out=factor[:], in0=factor[:], scalar=float(DIM) ** 0.5, in1=rstd,
                        op0=ALU.mult, op1=ALU.mult))
                    rstd = factor[:]
                for t in range(NT):
                    last = nc.vector.tensor_scalar(xn[:, t], src[:, t], mean_var[:, t, 0:1], rstd[:, t:t + 1],
                                                   ALU.subtract, ALU.mult)
                last.then_inc(xn_ready, 1)
                c["LN"] += 1

            def lo(dst, src, hi):
                dve.wait_ge(t_hi, turn.at(t_hi, c["T"] + 1))
                nc.vector.tensor_tensor(dst, src, hi.bitcast(F32), ALU.subtract).then_inc(t_lo, 1)
                c["T"] += 1

            def x_lo(dst, job):
                lo(dst[1][:].rearrange("p k s -> p (k s)"), bank[T_BANK[job]][:], dst[0][:].rearrange("p k s -> p (k s)"))

            def q_lo(t, i):
                dve.wait_ge(t_hi, turn.at(t_hi, c["T"] + 1))
                src = bank[T_BANK["q", t, i]][:].rearrange("p (a s) -> p a s", a=4)
                for odd in range(2):
                    rows, other = slice(DH * odd, DH * odd + DH), slice(DH - DH * odd, 2 * DH - DH * odd)
                    heads = slice(8 * i + odd, 8 * i + 8, 2)
                    last = nc.vector.tensor_tensor(q_t[other, t, heads, :], src[rows],
                                                   q_t[rows, t, heads, :].bitcast(F32), ALU.subtract)
                last.then_inc(t_lo, 1)
                c["T"] += 1

            def k_lo(t):
                lo(k_t[1][:, :, t * P:t * P + P],
                   bank[T_BANK["q", t, 2]][:].rearrange("p (h s) -> p h s", h=KV_HEADS),
                   k_t[0][:, :, t * P:t * P + P])

            def p_lo(n):
                for kb in range(key_blocks(n)):
                    lo(p_t[1][:, kb], bank[T_BANK["p", n, kb]][:], p_t[0][:, kb])

            def rope_products(t, i):
                slot, b = c["Q"] % 2, bank[Q_BANKS[i]]
                heads, half = (8 if i < 2 else KV_HEADS), DH // 2
                src = b[:, 0:heads * DH].rearrange("p (h d) -> p h d", h=heads)
                dve.wait_ge(q_ready, turn.at(q_ready, c["Q"] + 1))
                dve.wait_ge(rope_sum, turn.at(rope_sum, c["Q"] - 1))
                nc.vector.tensor_tensor(rope_c[:, slot, 0:heads], src,
                                        rope_sb[:, t, 0].unsqueeze(1).broadcast_to([P, heads, DH]), ALU.mult)
                for s in range(2):
                    to, of = slice(half * s, half * s + half), slice(half - half * s, DH - half * s)
                    last = nc.vector.tensor_tensor(rope_s[:, slot, 0:heads, to], src[:, :, of],
                                                   rope_sb[:, t, 1, to].unsqueeze(1).broadcast_to([P, heads, half]),
                                                   ALU.mult)
                last.then_inc(rope_mul, 1)
                c["Q"] += 1
                if i == 2:
                    vals = b[:, KV_HEADS * DH:2 * KV_HEADS * DH].rearrange("p (a e d) -> p a e d", a=2, e=2)
                    pair = v_halves[:, t].rearrange("p (a e) (s d) -> p a (e s) d", a=2, s=2)
                    settle(nc.vector.tensor_copy(pair[:, :, 0:4:3], vals))
                    nc.vector.tensor_tensor(pair[:, :, 1:3], vals, pair[:, :, 0:4:3].bitcast(F32), ALU.subtract
                                            ).then_inc(v_done, 1)

            def mask_max(pair):
                slot, keys = c["S"] % 4, P * key_blocks(c["S"] % GROUPS)
                value = turn.apart(dve, s_ready, 2 * c["S"] + pair + 1)
                dve.wait_ge(eye_in, 16)
                dve.wait_ge(s_ready, value)
                for g in range(2 * pair, 2 * pair + 2):
                    last = nc.vector.tensor_tensor_reduce(
                        probs[:, slot, g, 0:keys], bank[S_BANKS[pair]][:, g % 2 * SEQ:g % 2 * SEQ + keys],
                        mask_sb[:, SEQ - keys:SEQ], 1.0, -3.4e38, ALU.add, ALU.max, row_max[:, slot, g:g + 1])
                last.then_inc(s_used, 1)
                if pair:
                    dve.wait_ge(s_used, turn.at(s_used, 2 * c["S"] + 2))
                    nc.vector.tensor_scalar(neg_max[:, slot], row_max[:, slot], -DH ** -0.5, None, ALU.mult
                                            ).then_inc(s_max, 1)
                    c["S"] += 1

            def inverse():
                slot = c["R"] % 4
                dve.wait_ge(e_done, turn.at(e_done, c["R"] + 1))
                nc.vector.reciprocal(inv_sum[:, slot], row_sum[:, slot]).then_inc(r_done, 1)
                c["R"] += 1

            def add_large_half(n):
                rows = slice(DH * (n % 2), DH * (n % 2) + DH)
                dve.wait_ge(o_small, turn.at(o_small, c["V"] + 1))
                nc.vector.tensor_tensor(o_sums[rows], o_sums[rows], bank[O_BANK][rows], ALU.add).then_inc(o_sum, 1)
                c["V"] += 1

            def attention_residual(t):
                dve.wait_ge(y_ready, turn.at(y_ready, c["Y"] + 1))
                dve.wait_ge(x1_kept, turn.at(x1_kept, c["X"]))
                dve.wait_ge(d_used, turn.at(d_used, c["D"]))
                nc.vector.tensor_tensor(x2[:, t], bank[Y_BANKS[t]][:, 0:DIM], x1[:, t], ALU.add
                                        ).then_inc(y_used, 1)
                c["Y"] += 1

            def gate_product():
                slot = c["F"] % 2
                dve.wait_ge(th_done, turn.at(th_done, c["F"] + 1))
                nc.vector.scalar_tensor_tensor(out=hid[:, slot], in0=hid[:, slot], scalar=1.0, in1=bank[G_BANK][:],
                                               op0=ALU.add, op1=ALU.mult).then_inc(gate_used, 1)

            def up_product():
                slot = c["F"] % 2
                dve.wait_ge(u_ready, turn.at(u_ready, c["F"] + 1))
                dve.wait_ge(gate_used, turn.at(gate_used, c["F"] + 1))
                nc.vector.tensor_tensor(hid[:, slot], hid[:, slot], bank[U_BANK][:], ALU.mult
                                        ).then_inc(mul_done, 1)
                c["F"] += 1

            def ffn_residual(dst, src):
                dve.wait_ge(dn_done, turn.at(dn_done, PAIRS * (c["D"] + 1)))
                if dst is x1_next:
                    dve.wait_ge(x1_kept, turn.at(x1_kept, c["X"]))
                else:
                    dve.wait_ge(x_sent, turn.at(x_sent, 16 + 16 * c["W"]))
                    c["W"] += 1
                nc.vector.scalar_tensor_tensor(
                    out=dst[:].rearrange("p t d -> p (t d)"), in0=bank[D_BANK][:], scalar=0.25,
                    in1=src[:].rearrange("p t d -> p (t d)"), op0=ALU.mult, op1=ALU.add
                ).then_inc(d_used, 1)
                c["D"] += 1

            def body(second, first):
                c["X"] += 1
                if first:
                    dve.wait_ge(x_loaded, turn.at(x_loaded, 16 * (c["X"] + 1)))
                    statistics(x_in)
                rope_products(0, 0)
                if first:
                    normal_rows(x_in, False)
                rope_products(0, 1), rope_products(0, 2)
                if first:
                    x_lo(xf_t, "first")
                q_lo(0, 0), rope_products(1, 0), q_lo(0, 1)
                if first:
                    gate_product()
                rope_products(1, 1)
                if first:
                    up_product()
                rope_products(1, 2), k_lo(0)
                if first:
                    gate_product()
                q_lo(1, 0)
                if first:
                    up_product()
                q_lo(1, 1), k_lo(1)
                if second:
                    dve.wait_ge(y_used, turn.at(y_used, c["Y"]))
                    statistics(x2)
                mask_max(0)
                if first:
                    gate_product()
                mask_max(1)
                if first:
                    up_product()
                mask_max(0)
                if second:
                    normal_rows(x2, False)
                inverse(), mask_max(1)
                if first:
                    gate_product()
                mask_max(0), mask_max(1), inverse()
                if second:
                    x_lo(xf_t, "second")
                p_lo(0), mask_max(0)
                if first:
                    up_product()
                inverse(), mask_max(1), add_large_half(0), p_lo(1), mask_max(0), inverse(), mask_max(1)
                if second:
                    gate_product()
                add_large_half(1), p_lo(2)
                if second:
                    up_product()
                mask_max(0), mask_max(1), inverse(), p_lo(3), add_large_half(2), mask_max(0)
                if second:
                    gate_product()
                mask_max(1), inverse(), add_large_half(3), p_lo(4)
                if second:
                    up_product()
                mask_max(0)
                if first:
                    ffn_residual(x1_next, x_in)
                inverse(), mask_max(1), add_large_half(4), p_lo(5)
                if second:
                    gate_product(), up_product()
                inverse(), add_large_half(5), p_lo(6)
                if first:
                    dve.wait_ge(d_used, turn.at(d_used, c["D"]))
                    statistics(x1_next)
                if second:
                    gate_product()
                add_large_half(6), p_lo(7)
                if second:
                    up_product()
                if first:
                    normal_rows(x1_next, True)
                add_large_half(7)
                if second:
                    ffn_residual(y_out, x2)
                attention_residual(0)
                if first:
                    x_lo(xa_t, "attention")
                attention_residual(1)

            dve.wait_ge(x_loaded, turn.at(x_loaded, 16))
            statistics(x_in)
            split_lo(0), split_lo(1)
            normal_rows(x_in, False)
            split_lo(2), split_lo(3)
            x_lo(xf_t, "first")
            split_lo(4), split_lo(5)
            for p in range(PAIRS):
                gate_product(), up_product()
                split_lo(W_DOWN + p)
            for i in range(W_DOWN + PAIRS, W_ALL):
                split_lo(i)
            ffn_residual(x1_next, x_in)
            dve.wait_ge(d_used, turn.at(d_used, c["D"]))
            statistics(x1_next)
            normal_rows(x1_next, True)
            x_lo(xa_t, "attention")
            dve.wait_ge(rope_in, turn.at(rope_in, 16))
            dve.wait_ge(x_sent, turn.at(x_sent, 16))
            body(0, 1)
            before = dict(c)
            with dve.Fori(1, BATCH - 1) as turn.now:
                body(1, 1)
            turn.now = None
            after_loop(c, before, per_turn, BATCH - 2)
            body(1, 0)
            dve.wait_ge(y_used, turn.at(y_used, c["Y"]))
            statistics(x2)
            normal_rows(x2, False)
            x_lo(xf_t, "second")
            for p in range(PAIRS):
                gate_product(), up_product()
            ffn_residual(y_out, x2)

        @block.tensor
        def _(pe):
            turn, per_turn = Turn(raised), dict(T=JOBS["T"], Q=JOBS["Q"], S=JOBS["S"], O=JOBS["V"], Y=JOBS["Y"],
                                        F=JOBS["F"], DN=JOBS["F"], D=JOBS["D"], LN=JOBS["LN"], V=NT,
                                        t2=JOBS["T"], t3=JOBS["T"])
            c = tally(**per_turn, qk=0, ff=0, p=0)

            def product(dst, a, b, start, stop, shared=False):
                for i, (x, y) in enumerate(((0, 0), (0, 1), (1, 0))):
                    last = nc.tensor.matmul(dst, a[x], b[y], start=start and i == 0, stop=stop and i == 2,
                                            skip_group_check=shared)
                return last

            def transposes(job, blocks):
                b = T_BANK[job]
                pe.wait_ge(t_lo, turn.at(t_lo, c["t2"] if b == T_BANKS[0] else c["t3"]))
                for i, block_in in enumerate(blocks):
                    last = nc.tensor.transpose(bank[b][:, i * P:i * P + P], block_in, eye_sb[:])
                last.then_inc(t_ready, 1)
                c["T"] += 1
                if b == T_BANKS[0]:
                    c["t2"] = c["T"]
                else:
                    c["t3"] = c["T"]

            def x_transposes(job):
                pe.wait_ge(xn_ready, turn.at(xn_ready, c["LN"] + 1))
                transposes(job, [xn[:, t, k * P:k * P + P] for k in range(KC) for t in range(NT)])
                c["LN"] += 1

            def ffn_transposes(job):
                x_transposes(job)
                c["ff"] = c["T"]

            def q_transposes(t, i):
                pe.wait_ge(rope_sum, turn.at(rope_sum, c["Q0"] + 3 * t + i + 1))
                if i < 2:
                    transposes(("q", t, i), [q_rot[:, i, a * P:a * P + P] for a in range(4)])
                else:
                    transposes(("q", t, i), [k_rot[:, j].rearrange("p c d -> p (c d)") for j in range(KV_HEADS)])
                    c["qk"] = c["T"]

            def qkv(t, i):
                if t == 0 and i == 0:
                    pe.wait_ge(t_lo, turn.at(t_lo, c["T"]))
                if t == 0 and i < 2:
                    pe.wait_ge(y_used, turn.at(y_used, c["Y"] - 1 + i))
                elif t == 1 and i < 2:
                    pe.wait_ge(rope_mul, turn.at(rope_mul, c["Q"] - 2))
                elif t == 1:
                    pe.wait_ge(v_done, turn.at(v_done, c["V"]))
                rows = slice(t * P, t * P + P)
                for k in range(KC):
                    last = product(bank[Q_BANKS[i]][:], [x[:, k, rows] for x in xa_t],
                                   [w[:, k, 512 * i:512 * i + 512] for w in qkv_w], k == 0, k == KC - 1)
                last.then_inc(q_ready, 1)
                c["Q"] += 1
                c["V"] += i == 2

            def scores(pair):
                n = c["S"] % GROUPS
                t, j = n // KV_HEADS, n % KV_HEADS
                pe.wait_ge(t_lo, turn.at(t_lo, c["qk"]))
                pe.wait_ge(s_used, turn.at(s_used, 2 * c["S"] - 1 + pair))
                for g in range(2 * pair, 2 * pair + 2):
                    dst = bank[S_BANKS[pair]][:, g % 2 * SEQ:g % 2 * SEQ + SEQ]
                    for s in range(2):
                        last = nc.tensor.matmul(dst, q_t[:, t, KV_HEADS * g + j, :], k_t[s][:, j, :],
                                                start=s == 0, stop=s == 1)
                last.then_inc(s_ready, 1)
                c["S"] += pair

            def p_transposes(n):
                pe.wait_ge(p_done, turn.at(p_done, c["P0"] + n + 1))
                for kb in range(key_blocks(n)):
                    transposes(("p", n, kb), [probs[:, n % 4, g, kb * P:kb * P + P] for g in range(GROUP)])
                c["p"] = c["T"]

            def values(n):
                t, j = n // KV_HEADS, n % KV_HEADS
                pe.wait_ge(t_lo, turn.at(t_lo, c["p"]))
                if n == 0:
                    pe.wait_ge(v_done, turn.at(v_done, c["V"]))
                else:
                    pe.wait_ge(o_sum, turn.at(o_sum, c["O"]))
                for kb in range(t + 1):
                    for s in range(2):
                        last = nc.tensor.matmul(bank[O_BANK][:], v_halves[:, kb, j], p_t[s][:, kb],
                                                start=kb == 0 and s == 0, stop=kb == t and s == 1)
                last.then_inc(o_ready, 1)
                c["O"] += 1

            def projection(t):
                pe.wait_ge(o_lo, turn.at(o_lo, c["O0"] // 2 + 2 * (t + 1)))
                pe.wait_ge(s_used, turn.at(s_used, 2 * c["S"]))
                for k in range(OC):
                    last = product(bank[Y_BANKS[t]][:, 0:DIM], [o[:, t, k % 2, k // 2] for o in o_t],
                                   [w[:, k] for w in out_w], k == 0, k == OC - 1)
                last.then_inc(y_ready, 1)
                c["Y"] += 1

            def hidden_product(weight, b):
                for h in range(2):
                    cols = slice((2 * (c["F"] % PAIRS) + h) * P, (2 * (c["F"] % PAIRS) + h + 1) * P)
                    for k in range(KC):
                        last = product(bank[b][:, h * SEQ:h * SEQ + SEQ], [w[:, k, cols] for w in weight],
                                       [x[:, k] for x in xf_t], k == 0, k == KC - 1)
                return last

            def gate():
                pe.wait_ge(t_lo, turn.at(t_lo, c["ff"]))
                pe.wait_ge(gate_used, turn.at(gate_used, c["F"]))
                hidden_product(gate_w, G_BANK).then_inc(g_ready, 1)

            def up():
                pe.wait_ge(mul_done, turn.at(mul_done, c["F"]))
                hidden_product(up_w, U_BANK).then_inc(u_ready, 1)
                c["F"] += 1

            def down():
                p, slot = c["DN"] % PAIRS, c["DN"] % 2
                pe.wait_ge(h_lo, turn.at(h_lo, c["DN"] + 1))
                if p == 0:
                    pe.wait_ge(d_used, turn.at(d_used, c["D"]))
                for t in range(NT):
                    for h in range(2):
                        last = product(bank[D_BANK][:, t * DIM:t * DIM + DIM],
                                       [x[:, slot, h, t * P:t * P + P] for x in (hid_hi, hid_lo)],
                                       [w[:, 2 * p + h] for w in down_w],
                                       p == 0 and t == 0 and h == 0, p == PAIRS - 1 and t == NT - 1 and h == 1,
                                       shared=True)
                last.then_inc(dn_done, 1)
                c["DN"] += 1
                if p == PAIRS - 1:
                    c["D"] += 1

            def body(second, first):
                c["P0"], c["Q0"], c["O0"] = c["S"], c["Q"], c["O"]
                qkv(0, 0), qkv(0, 1), qkv(0, 2)
                if first:
                    ffn_transposes("first")
                q_transposes(0, 0), qkv(1, 0), qkv(1, 1), q_transposes(0, 1)
                if first:
                    gate(), up()
                q_transposes(0, 2), qkv(1, 2)
                if first:
                    gate()
                q_transposes(1, 0)
                if first:
                    up()
                q_transposes(1, 1)
                if first:
                    gate()
                q_transposes(1, 2)
                if first:
                    down(), up()
                scores(0), scores(1), scores(0)
                if first:
                    gate()
                scores(1)
                if first:
                    up()
                scores(0)
                if second:
                    ffn_transposes("second")
                scores(1), p_transposes(0), scores(0)
                if first:
                    down()
                scores(1), values(0), scores(0), p_transposes(1)
                if second:
                    gate()
                scores(1), values(1)
                if second:
                    up()
                p_transposes(2), scores(0)
                if second:
                    gate()
                values(2), scores(1), p_transposes(3)
                if second:
                    up()
                scores(0)
                if first:
                    down()
                values(3), scores(1), p_transposes(4), scores(0)
                if second:
                    gate()
                if first:
                    down()
                values(4), scores(1), p_transposes(5)
                if second:
                    up(), down()
                values(5), p_transposes(6)
                if second:
                    down(), gate()
                values(6), p_transposes(7)
                if second:
                    up(), down()
                values(7), projection(0)
                if first:
                    x_transposes("attention")
                if second:
                    down()
                projection(1)

            pe.wait_ge(eye_in, turn.at(eye_in, 16))
            ffn_transposes("first")
            pe.wait_ge(w_lo, turn.at(w_lo, W_GATE_UP))
            gate(), up()
            gate(), up()
            pe.wait_ge(w_lo, turn.at(w_lo, W_DOWN))
            down()
            gate(), up()
            down()
            gate(), up()
            down()
            down()
            x_transposes("attention")
            pe.wait_ge(w_lo, turn.at(w_lo, W_ALL))
            body(0, 1)
            before = dict(c)
            with pe.Fori(1, BATCH - 1) as turn.now:
                body(1, 1)
            turn.now = None
            after_loop(c, before, per_turn, BATCH - 2)
            body(1, 0)
            ffn_transposes("second")
            gate(), up()
            for _ in range(PAIRS - 1):
                gate(), up()
                down()
            down()


_INS = ["x", "w_gate", "w_up", "w_down", "w_qkv", "w_out", "gamma", "rope", "mask", "eye"]


def _chunks(w):
    return np.ascontiguousarray(w.reshape(w.shape[0] // P, P, w.shape[1]).transpose(1, 0, 2))


def _rope_table():
    inv = np.float32(10000.0) ** -(np.arange(0, DH, 2, dtype=np.float32) / np.float32(DH))
    angle = (np.arange(SEQ, dtype=np.float32)[:, None] * inv[None, :].astype(np.float32)).astype(np.float64)
    cos, sin = np.cos(angle), np.sin(angle)
    table = np.stack([np.concatenate([cos, cos], 1), np.concatenate([-sin, sin], 1)], 1)
    return np.ascontiguousarray(table.reshape(NT, P, 2, DH).transpose(1, 0, 2, 3).astype(np.float32))


def kernel(L0_attn_x, L0_attn_gamma, L0_attn_w_qkv, L0_attn_w_out, L0_ffn_w_gate, L0_ffn_w_up, L0_ffn_w_down):
    import concourse.bacc as _bacc
    from concourse.bass_utils import run_bass_kernel_spmd as _run

    causal = np.where(np.tril(np.ones((P, P), bool)), 0.0, MASKED).astype(np.float32)
    given = {
        "x": np.ascontiguousarray(L0_attn_x),
        "w_gate": _chunks(np.asarray(L0_ffn_w_gate).T),
        "w_up": _chunks(np.asarray(L0_ffn_w_up).T),
        "w_down": _chunks(np.asarray(L0_ffn_w_down).T),
        "w_qkv": _chunks(np.asarray(L0_attn_w_qkv)),
        "w_out": _chunks(np.asarray(L0_attn_w_out)),
        "gamma": np.ascontiguousarray(np.asarray(L0_attn_gamma).reshape(KC, P).T),
        "rope": _rope_table(),
        "mask": np.concatenate([np.zeros((P, SEQ - P), np.float32), causal], 1),
        "eye": np.eye(P, dtype=np.float32),
    }
    nc = _bacc.Bacc("TRN2", target_bir_lowering=False, num_devices=1)
    args = [nc.dram_tensor(f"in_{n}", given[n].shape, F32, kind="ExternalInput").ap() for n in _INS]
    out = nc.dram_tensor("out_0", (BATCH, SEQ, DIM), F32, kind="ExternalOutput").ap()
    build(nc, *args, out)
    r = _run(nc, [{f"in_{n}": given[n] for n in _INS}], core_ids=[0])
    return r.results[0]["out_0"]
```

```python
import numpy as np
import concourse.bass as bass
from concourse import mybir
from contextlib import ExitStack

F32 = mybir.dt.float32
F32R = mybir.dt.float32r
ALU = mybir.AluOpType
ACT = mybir.ActivationFunctionType

BATCH, SEQ, DIM = 8, 256, 256
HEADS, KV_HEADS, DH = 16, 4, 64
GROUP = HEADS // KV_HEADS
HID = 1024
P = 128
NT = SEQ // P
KC = DIM // P
QKV = (HEADS + 2 * KV_HEADS) * DH
PAIRS = HID // (2 * P)
OC = HEADS * DH // P
MASKED = -3.0e38
EPS = 1e-5
NORM_MIN = 1e-12
GROUPS = NT * KV_HEADS


def key_blocks(n):
    return n // KV_HEADS + 1


TRANSPOSES = dict(opening=22, turn=21, ending=20)
TILE0_DONE = dict(opening=(5, 6, 7), turn=(2, 4, 3), ending=(1, 2, 3))


class Turn:

    def __init__(self, per_turn):
        self.per_turn, self.now = per_turn, None

    def at(self, semaphore, count):
        if self.now is None:
            return max(count, 0)
        per_turn = self.per_turn[semaphore.name]
        assert count > 0 and per_turn
        return (self.now - 1) * per_turn + count

    def apart(self, engine, semaphore, count):
        value = self.at(semaphore, count)
        return value if self.now is None else engine.to_reg(value)


def tally(**kinds):
    return {kind: 0 for kind in kinds}


def after_loop(c, before, per_turn, turns):
    for kind, n in per_turn.items():
        assert c[kind] - before[kind] == n, (kind, c[kind] - before[kind])
        c[kind] += (turns - 1) * n


JOBS = dict(T=TRANSPOSES["turn"], Q=6, S=GROUPS, V=GROUPS, OT=GROUPS // 2, Y=NT, F=2 * PAIRS, D=2, LN=3, X=1)




def build(nc, x, w_gate, w_up, w_down, w_qkv, w_out, gamma, rope, mask, eye, out):
    ctx = ExitStack()
    with ctx:
        def sb(name, shape, dt=F32):
            return ctx.enter_context(nc.sbuf_tensor(name, shape, dt))

        raised = {}

        def sig(name, per_turn=0):
            semaphore = ctx.enter_context(nc.semaphore(name))
            raised[semaphore.name] = per_turn
            return semaphore

        gate_w = [sb(f"gate_{s}", [P, KC, HID], F32R) for s in ("hi", "lo")]
        up_w = [sb(f"up_{s}", [P, KC, HID], F32R) for s in ("hi", "lo")]
        down_w = [sb(f"down_{s}", [P, HID // P, DIM], F32R) for s in ("hi", "lo")]
        qkv_w = [sb(f"qkv_{s}", [P, KC, QKV], F32R) for s in ("hi", "lo")]
        out_w = [sb(f"out_{s}", [P, OC, DIM], F32R) for s in ("hi", "lo")]
        gamma_sb = sb("gamma_sb", [P, KC])
        rope_sb = sb("rope_sb", [P, NT, 2, DH])
        mask_sb = sb("mask_sb", [P, SEQ])
        eye_sb = sb("eye_sb", [P, P])
        exponent = sb("exponent", [P, 2, NT])

        x_in = sb("x_in", [P, NT, DIM])
        x1_next = sb("x1_next", [P, NT, DIM])
        x1 = sb("x1", [P, NT, DIM])
        x2 = sb("x2", [P, NT, DIM])
        y_out = sb("y_out", [P, NT, DIM])
        xn = sb("xn", [P, NT, DIM])
        xf_t = [sb(f"xf_t_{s}", [P, KC, SEQ], F32R) for s in ("hi", "lo")]
        xa_t = [sb(f"xa_t_{s}", [P, KC, SEQ], F32R) for s in ("hi", "lo")]
        stats = sb("stats", [P, NT, 6])
        mean_var = sb("mean_var", [P, NT, 2])
        power_in = sb("power_in", [P, 2, NT])
        power_out = sb("power_out", [P, 2, NT])
        factor = sb("factor", [P, NT])

        hid = sb("hid", [P, 2, 2 * P * NT])
        hid_hi = sb("hid_hi", [P, 2, 2, SEQ], F32R)
        hid_lo = sb("hid_lo", [P, 2, 2, SEQ], F32R)

        q_rot = sb("q_rot", [P, 2, 8 * DH])
        k_rot = sb("k_rot", [P, KV_HEADS, 2, DH])
        q_t = sb("q_t", [P, NT, HEADS, P], F32R)
        k_t = sb("k_t", [P, KV_HEADS, 2, SEQ], F32R)
        v_halves = sb("v_halves", [P, NT, KV_HEADS, 2 * DH], F32R)
        probs = sb("probs", [P, 4, GROUP, SEQ])
        row_max = sb("row_max", [P, 4, GROUP])
        neg_max = sb("neg_max", [P, 4, GROUP])
        row_sum = sb("row_sum", [P, 4, GROUP])
        inv_sum = sb("inv_sum", [P, 4, GROUP])
        with nc.sbuf_tensor("rope_c", [P, 2, 8, DH], F32) as rope_c:
            with nc.sbuf_tensor("rope_s", [P, 2, 8, DH], F32) as rope_s:
                pass
        p_odd = [sb(f"p_odd_{s}", [P, NT, GROUP * P], F32R) for s in ("hi", "lo")]
        p_even = [sb(f"p_even_{s}", [P, NT, GROUP * P], F32R) for s in ("hi", "lo")]
        p_t = [p_even, p_odd]
        o_sums = sb("o_sums", [P, GROUP * P])
        o_t = [sb(f"o_t_{s}", [P, NT, 2, GROUP, P], F32R) for s in ("hi", "lo")]

        bank = [ctx.enter_context(nc.psum_tensor(f"bank{i}", [P, 512], F32)) for i in range(8)]
        Q_BANKS, S_BANKS, Y_BANKS, T_BANKS = (0, 1, 4), (0, 1), (0, 1), (2, 3)
        O_BANK, G_BANK, U_BANK, D_BANK = 4, 5, 6, 7

        def t_bank(c):
            return bank[T_BANKS[(c["T"] - c["T0"]) % 2]]

        eye_in, gamma_in, rope_in = sig("eye_in"), sig("gamma_in"), sig("rope_in")
        w_in = [sig(f"w_in{i}") for i in range(4)]
        w_hi, w_lo, w_lo_pool = sig("w_hi"), sig("w_lo"), sig("w_lo_pool")
        exponents_set, zeros_set = sig("exponents_set"), sig("zeros_set")
        x0_loaded, x_loaded = sig("x0_loaded"), sig("x_loaded", 16)
        x_sent = sig("x_sent", 16)
        x1_kept = sig("x1_kept", 1)
        ln_var = sig("ln_var", JOBS["LN"])
        ln_pow = sig("ln_pow", JOBS["LN"])
        xn_ready = sig("xn_ready", JOBS["LN"])
        t_ready, t_hi, t_lo = (sig(n, JOBS["T"]) for n in ("t_ready", "t_hi", "t_lo"))
        q_ready = sig("q_ready", 6)
        rope_mul, rope_sum = sig("rope_mul", 6), sig("rope_sum", 6)
        v_done = sig("v_done", NT)
        s_ready, s_used = sig("s_ready", 2 * GROUPS), sig("s_used", 2 * GROUPS)
        low_copied, low_masked = (sig(n, 2 * KV_HEADS) for n in ("low_copied", "low_masked"))
        s_max, e_done, r_done, p_done = (sig(n, GROUPS) for n in ("s_max", "e_done", "r_done", "p_done"))
        o_ready, o_small, o_sum = (sig(n, JOBS["V"]) for n in ("o_ready", "o_small", "o_sum"))
        o_hi, o_lo = (sig(n, JOBS["OT"]) for n in ("o_hi", "o_lo"))
        y_ready, y_used = sig("y_ready", NT), sig("y_used", NT)
        g_ready, u_ready, th_done, gate_used, mul_done, h_hi, h_lo, dn_done = (
            sig(n, JOBS["F"]) for n in
            ("g_ready", "u_ready", "th_done", "gate_used", "mul_done", "h_hi", "h_lo", "dn_done"))
        d_used = sig("d_used", JOBS["D"])
        DVE_OWN = 3 * 2 + 4 + NT
        dve_own = sig("dve_own", DVE_OWN)

        def piece(w, dst, part, k=None):
            return w[part], [d[part] for d in dst], k

        every, width = slice(None), QKV // 2
        halves = [slice(0, HID // 2), slice(HID // 2, HID)]
        chunk_halves = [slice(0, HID // P // 2), slice(HID // P // 2, HID // P)]
        pieces = [piece(w, dst, (every, every, h)) for h in halves for w, dst in ((w_gate, gate_w), (w_up, up_w))]
        pieces += [piece(w_down, down_w, (every, h, every)) for h in chunk_halves]
        pieces += [piece(w_qkv, qkv_w, (every, slice(k, k + 1), slice(i, i + width)), k)
                   for k in range(KC) for i in (0, width)]
        pieces += [piece(w_out, out_w, (every, h, every)) for h in chunk_halves]
        W_GATE_UP, W_QKV, W_ALL = 4, 6 + 2 * KC, len(pieces)

        ON_POOL = [i for i in range(W_GATE_UP, W_ALL) if pieces[i][2] is None]

        def lo_done(i):
            before = sum(j <= i for j in ON_POOL)
            return (w_lo_pool, before) if i in ON_POOL else (w_lo, i + 1 - before)

        def stage(i):
            _, a, n = pieces[i][0].shape
            return probs[:, i % 4].rearrange("p g k -> p (g k)")[:, 0:a * n].rearrange("p (a n) -> p a n", a=a)

        block = ctx.enter_context(nc.Block())

        @block.sync
        def _(sp):
            turn = Turn(raised)

            def rows(array, m):
                return array[bass.ds(m, 1)].rearrange("o (t p) d -> p (o t) d", p=P)

            sp.dma_start(x2[:], rows(x, 0)).then_inc(x0_loaded, 16)
            for i, (src, _, _) in enumerate(pieces):
                if i >= 4:
                    sp.wait_ge(*lo_done(i - 4))
                sp.dma_start(stage(i), src).then_inc(w_in[i % 4], 16)
                if i == 0:
                    sp.dma_start(eye_sb[:], eye).then_inc(eye_in, 16)
                    sp.dma_start(gamma_sb[:], gamma).then_inc(gamma_in, 16)
                if i == W_GATE_UP - 1:
                    sp.dma_start(x_in[:], rows(x, 1)).then_inc(x_loaded, 16)
                if i == W_QKV - 1:
                    sp.dma_start(rope_sb[:], rope).then_inc(rope_in, 16)
                    sp.dma_start(mask_sb[:], mask).then_inc(x_sent, 16)
            sp.wait_ge(d_used, turn.at(d_used, 2))
            sp.dma_start(x_in[:], rows(x, 2)).then_inc(x_loaded, 16)
            with sp.Fori(1, BATCH - 2) as turn.now:
                sp.wait_ge(d_used, turn.at(d_used, 3))
                sp.dma_start(x_in[:], rows(x, turn.now + 2)).then_inc(x_loaded, 16)
                sp.wait_ge(d_used, turn.at(d_used, 4))
                sp.dma_start(rows(out, turn.now - 1), y_out[:]).then_inc(x_sent, 16)
            turn.now = None
            used = 2 + 2 * (BATCH - 3)
            for m, more in ((BATCH - 3, 2), (BATCH - 2, 3), (BATCH - 1, 4)):
                sp.wait_ge(d_used, turn.at(d_used, used + more))
                sp.dma_start(rows(out, m), y_out[:]).then_inc(x_sent, 16)
            sp.wait_ge(x_sent, turn.at(x_sent, 16 + 16 * BATCH))

        @block.gpsimd
        def _(pool):
            turn, per_turn = Turn(raised), dict(T=JOBS["T"], Q=JOBS["Q"], S=JOBS["S"], F=JOBS["F"], LN=JOBS["LN"],
                                                OT=JOBS["OT"], LM=2 * KV_HEADS)
            c = tally(**per_turn, T0=0)
            nc.gpsimd.memset(exponent[:, 0], -0.5).then_inc(exponents_set, 1)
            nc.gpsimd.memset(exponent[:, 1], 0.5).then_inc(exponents_set, 1)
            pool.wait_ge(exponents_set, turn.at(exponents_set, 2))

            def split_lo(i):
                pool.wait_ge(w_hi, turn.at(w_hi, i + 1))
                _, dst, _ = pieces[i]
                nc.gpsimd.tensor_tensor(dst[1], stage(i), dst[0].bitcast(F32), ALU.subtract).then_inc(w_lo_pool, 1)

            def powers():
                pool.wait_ge(ln_var, turn.at(ln_var, c["LN"] + 1))
                nc.gpsimd.tensor_tensor(power_out[:], power_in[:], exponent[:], ALU.pow
                                        ).then_inc(ln_pow, 1)
                c["LN"] += 1

            def rope_add(part, t, i):
                slot = c["Q"] % 2
                pool.wait_ge(rope_mul, turn.at(rope_mul, c["Q"] + 1))
                pool.wait_ge(t_ready, turn.at(t_ready, c["T0"] + (TILE0_DONE[part][i] if t else 0)))
                if i < 2:
                    nc.gpsimd.tensor_tensor(
                        q_rot[:, i], rope_c[:, slot].rearrange("p h d -> p (h d)"),
                        rope_s[:, slot].rearrange("p h d -> p (h d)"), ALU.add).then_inc(rope_sum, 1)
                else:
                    for copy in range(2):
                        last = nc.gpsimd.tensor_tensor(
                            k_rot[:, :, copy, :], rope_c[:, slot, 0:KV_HEADS],
                            rope_s[:, slot, 0:KV_HEADS], ALU.add)
                    last.then_inc(rope_sum, 1)
                c["Q"] += 1

            def low_mask():
                n, pair = c["LM"] // 2 % KV_HEADS, c["LM"] % 2
                pool.wait_ge(low_copied, turn.at(low_copied, c["LM"] + 1))
                part = probs[:, n, 2 * pair:2 * pair + 2, 0:P]
                nc.gpsimd.tensor_tensor(part, part, mask_sb[:, SEQ - P:].unsqueeze(1).broadcast_to([P, 2, P]), ALU.add
                                        ).then_inc(low_masked, 1)
                c["LM"] += 1

            def normalise():
                slot, keys = c["S"] % 4, P * key_blocks(c["S"] % GROUPS)
                pool.wait_ge(r_done, turn.at(r_done, c["S"] + 1))
                part = probs[:, slot, :, 0:keys]
                nc.gpsimd.tensor_tensor(
                    part, part, inv_sum[:, slot].unsqueeze(2).broadcast_to([P, GROUP, keys]),
                    ALU.mult).then_inc(p_done, 1)
                c["S"] += 1

            def hidden_lo():
                slot = c["F"] % 2
                pool.wait_ge(h_hi, turn.at(h_hi, c["F"] + 1))
                pool.wait_ge(dn_done, turn.at(dn_done, c["F"] - 1))
                nc.gpsimd.tensor_tensor(
                    hid_lo[:, slot].rearrange("p c n -> p (c n)"), hid[:, slot],
                    hid_hi[:, slot].rearrange("p c n -> p (c n)").bitcast(F32),
                    ALU.subtract).then_inc(h_lo, 1)
                c["F"] += 1

            def outputs_lo():
                t, jp = c["OT"] // 2 % NT, c["OT"] % 2
                pool.wait_ge(o_hi, turn.at(o_hi, c["OT"] + 1))
                nc.gpsimd.tensor_tensor(
                    o_t[1][:, t, jp].rearrange("p g s -> p (g s)"), o_sums[:],
                    o_t[0][:, t, jp].rearrange("p g s -> p (g s)").bitcast(F32), ALU.subtract
                ).then_inc(o_lo, 1)
                c["OT"] += 1

            c["T0"] = -1
            powers(), powers(), split_lo(4), hidden_lo(), split_lo(5), hidden_lo(), hidden_lo(), hidden_lo()
            split_lo(10), powers(), split_lo(11), rope_add("opening", 0, 0), rope_add("opening", 0, 1), hidden_lo()
            rope_add("opening", 0, 2), hidden_lo(), rope_add("opening", 1, 0), rope_add("opening", 1, 1)
            pool.wait_ge(x_sent, turn.at(x_sent, 16))
            low_mask(), low_mask(), rope_add("opening", 1, 2), low_mask(), low_mask(), normalise(), low_mask()
            low_mask(), low_mask(), low_mask(), normalise(), hidden_lo(), normalise(), normalise(), normalise()
            outputs_lo(), normalise(), normalise(), hidden_lo(), outputs_lo(), normalise(), outputs_lo(), powers()
            outputs_lo()

            c["T"] += TRANSPOSES["opening"]

            before = dict(c)
            with pool.Fori(1, BATCH - 1) as turn.now:
                c["T0"] = c["T"]
                powers(), rope_add("turn", 0, 0), rope_add("turn", 0, 1), rope_add("turn", 0, 2), powers()
                rope_add("turn", 1, 0), hidden_lo(), low_mask(), rope_add("turn", 1, 1), low_mask(), hidden_lo()
                low_mask(), rope_add("turn", 1, 2), low_mask(), low_mask(), hidden_lo(), low_mask(), normalise()
                low_mask(), low_mask(), normalise(), normalise(), hidden_lo(), normalise(), normalise()
                outputs_lo(), hidden_lo(), normalise(), normalise(), outputs_lo(), hidden_lo(), normalise()
                hidden_lo(), outputs_lo(), powers(), hidden_lo(), outputs_lo()
                c["T"] += TRANSPOSES["turn"]
            turn.now = None
            after_loop(c, before, per_turn, BATCH - 2)

            c["T0"] = c["T"]
            powers(), rope_add("ending", 0, 0), rope_add("ending", 0, 1), rope_add("ending", 0, 2)
            rope_add("ending", 1, 0), low_mask(), low_mask(), rope_add("ending", 1, 1), low_mask(), low_mask()
            rope_add("ending", 1, 2), low_mask(), normalise(), low_mask(), normalise(), low_mask(), low_mask()
            normalise(), normalise(), outputs_lo(), normalise(), normalise(), normalise(), hidden_lo(), outputs_lo()
            normalise(), hidden_lo(), outputs_lo(), outputs_lo(), hidden_lo(), powers(), hidden_lo(), hidden_lo()
            hidden_lo(), hidden_lo(), hidden_lo()

        @block.scalar
        def _(act):
            turn, per_turn = Turn(raised), dict(T=JOBS["T"], S=JOBS["S"], V=JOBS["V"], OT=JOBS["OT"], F=JOBS["F"],
                                                H=JOBS["F"], Y=JOBS["Y"], D=JOBS["D"], LC=2 * KV_HEADS)
            c = tally(**per_turn, T0=0)

            def split_hi(i):
                act.wait_ge(w_in[i % 4], turn.at(w_in[i % 4], 16 * (i // 4 + 1)))
                _, dst, k = pieces[i]
                scale = 1.0
                if k is not None:
                    scale = gamma_sb[:, k:k + 1]
                    act.wait_ge(gamma_in, turn.at(gamma_in, 16))
                nc.scalar.activation(dst[0], stage(i), ACT.Copy, scale=scale).then_inc(w_hi, 1)

            def x_hi(dst):
                act.wait_ge(t_ready, turn.at(t_ready, c["T"] + 1))
                nc.scalar.activation(dst[0][:].rearrange("p k s -> p (k s)"), t_bank(c)[:], ACT.Copy
                                     ).then_inc(t_hi, 1)
                c["T"] += 1

            def q_hi(t, i):
                act.wait_ge(t_ready, turn.at(t_ready, c["T"] + 1))
                src = t_bank(c)[:].rearrange("p (a s) -> p a s", a=4)
                for odd in range(2):
                    rows = slice(DH * odd, DH * odd + DH)
                    last = nc.scalar.activation(q_t[rows, t, 8 * i + odd:8 * i + 8:2, :], src[rows], ACT.Copy)
                last.then_inc(t_hi, 1)
                c["T"] += 1

            def k_hi(t):
                act.wait_ge(t_ready, turn.at(t_ready, c["T"] + 1))
                nc.scalar.activation(k_t[:, :, 0, t * P:t * P + P],
                                     t_bank(c)[:].rearrange("p (h s) -> p h s", h=KV_HEADS), ACT.Copy
                                     ).then_inc(t_hi, 1)
                c["T"] += 1

            def p_hi(n, kb):
                act.wait_ge(t_ready, turn.at(t_ready, c["T"] + 1))
                nc.scalar.activation(p_t[n % 2][0][:, kb], t_bank(c)[:], ACT.Copy).then_inc(t_hi, 1)
                c["T"] += 1

            def keep_x1():
                act.wait_ge(y_used, turn.at(y_used, c["Y"]))
                act.wait_ge(d_used, turn.at(d_used, c["D"]))
                nc.scalar.activation(x1[:], x1_next[:], ACT.Copy).then_inc(x1_kept, 1)

            def low_copy():
                n, pair = c["LC"] // 2 % KV_HEADS, c["LC"] % 2
                act.wait_ge(s_ready, turn.at(s_ready, c["LC"] // (2 * KV_HEADS) * 2 * GROUPS + 2 * n + pair + 1))
                scores = bank[S_BANKS[pair]][:].rearrange("p (g s k) -> p g s k", g=2, s=2)
                nc.scalar.activation(probs[:, n, 2 * pair:2 * pair + 2, 0:P], scores[:, :, 1], ACT.Copy
                                     ).then_inc(low_copied, 1)
                c["LC"] += 1

            def exps():
                slot, keys = c["S"] % 4, P * key_blocks(c["S"] % GROUPS)
                act.wait_ge(s_max, turn.at(s_max, c["S"] + 1))
                for g in range(GROUP):
                    part = probs[:, slot, g, 0:keys]
                    last = nc.scalar.activation(part, part, ACT.Exp, bias=neg_max[:, slot, g:g + 1],
                                                scale=DH ** -0.5, accum_out=row_sum[:, slot, g:g + 1])
                last.then_inc(e_done, 1)
                c["S"] += 1

            def small_half(n):
                odd = n % 2
                act.wait_ge(o_ready, turn.at(o_ready, c["V"] + 1))
                if not odd:
                    act.wait_ge(o_lo, turn.at(o_lo, c["OT"]))
                rows, other = slice(DH * odd, DH * odd + DH), slice(DH - DH * odd, 2 * DH - DH * odd)
                nc.scalar.activation(o_sums[rows], bank[O_BANK][other], ACT.Copy).then_inc(o_small, 1)
                c["V"] += 1

            def outputs_hi():
                t, jp = c["OT"] // 2 % NT, c["OT"] % 2
                act.wait_ge(o_sum, turn.at(o_sum, 2 * c["OT"] + 2))
                nc.scalar.activation(o_t[0][:, t, jp].rearrange("p g s -> p (g s)"), o_sums[:], ACT.Copy
                                     ).then_inc(o_hi, 1)
                c["OT"] += 1

            def tanh():
                slot = c["F"] % 2
                act.wait_ge(g_ready, turn.at(g_ready, c["F"] + 1))
                act.wait_ge(h_lo, turn.at(h_lo, c["F"] - 1))
                nc.scalar.activation(hid[:, slot], bank[G_BANK][:], ACT.Tanh, scale=0.5
                                     ).then_inc(th_done, 1)
                c["F"] += 1

            def hidden_hi():
                slot = c["H"] % 2
                act.wait_ge(mul_done, turn.at(mul_done, c["H"] + 1))
                act.wait_ge(dn_done, turn.at(dn_done, c["H"] - 1))
                nc.scalar.activation(hid_hi[:, slot].rearrange("p c n -> p (c n)"), hid[:, slot], ACT.Copy
                                     ).then_inc(h_hi, 1)
                c["H"] += 1

            c["T0"], c["D"] = -1, 1
            split_hi(0), split_hi(1), x_hi(xf_t), split_hi(2), split_hi(3), tanh(), split_hi(4), hidden_hi(), tanh()
            split_hi(5), split_hi(6), hidden_hi(), tanh(), split_hi(7), split_hi(8), hidden_hi(), tanh()
            hidden_hi(), x_hi(xf_t), split_hi(9), split_hi(10), tanh(), keep_x1(), split_hi(11), hidden_hi(), tanh()
            x_hi(xa_t), hidden_hi(), q_hi(0, 0), q_hi(0, 1), k_hi(0), tanh(), low_copy(), low_copy(), q_hi(1, 1)
            q_hi(1, 0), low_copy(), low_copy(), exps(), k_hi(1), low_copy(), hidden_hi(), low_copy(), exps(), tanh()
            low_copy(), p_hi(0, 0), low_copy(), exps(), small_half(0), exps(), p_hi(1, 0), exps(), small_half(1)
            p_hi(2, 0), exps(), p_hi(3, 0), outputs_hi(), exps(), small_half(2), p_hi(4, 1), p_hi(4, 0), hidden_hi()
            small_half(3), p_hi(5, 1), p_hi(5, 0), outputs_hi(), exps(), small_half(4), p_hi(6, 1), p_hi(6, 0)
            small_half(5), p_hi(7, 0), outputs_hi(), p_hi(7, 1), small_half(6), small_half(7), outputs_hi()
            x_hi(xa_t)

            c["Y"] += NT
            c["D"] += 1

            before = dict(c)
            with act.Fori(1, BATCH - 1) as turn.now:
                c["T0"] = c["T"]
                x_hi(xf_t), keep_x1(), q_hi(0, 0), tanh(), k_hi(0), q_hi(0, 1), hidden_hi(), tanh(), low_copy()
                low_copy(), hidden_hi(), tanh(), low_copy(), q_hi(1, 0), exps(), low_copy(), hidden_hi(), low_copy()
                q_hi(1, 1), tanh(), low_copy(), exps(), x_hi(xf_t), low_copy(), k_hi(1), low_copy(), exps(), tanh()
                p_hi(0, 0), exps(), p_hi(1, 0), hidden_hi(), small_half(0), exps(), p_hi(2, 0), small_half(1)
                tanh(), p_hi(3, 0), hidden_hi(), outputs_hi(), exps(), small_half(2), p_hi(4, 1), p_hi(4, 0), exps()
                small_half(3), tanh(), hidden_hi(), p_hi(5, 1), outputs_hi(), p_hi(5, 0), exps(), small_half(4)
                p_hi(6, 1), tanh(), p_hi(6, 0), hidden_hi(), small_half(5), outputs_hi(), hidden_hi(), p_hi(7, 1)
                p_hi(7, 0), small_half(6), small_half(7), outputs_hi(), x_hi(xa_t)
                c["Y"] += NT
                c["D"] += JOBS["D"]
            turn.now = None
            after_loop(c, before, per_turn, BATCH - 2)

            c["T0"] = c["T"]
            keep_x1(), q_hi(0, 0), q_hi(0, 1), k_hi(0), x_hi(xf_t), low_copy(), low_copy(), q_hi(1, 0), low_copy()
            low_copy(), exps(), q_hi(1, 1), low_copy(), exps(), low_copy(), k_hi(1), tanh(), low_copy(), p_hi(0, 0)
            low_copy(), exps(), p_hi(1, 0), small_half(0), tanh(), exps(), p_hi(2, 0), small_half(1), exps()
            outputs_hi(), p_hi(3, 0), exps(), small_half(2), exps(), p_hi(4, 0), small_half(3), hidden_hi()
            p_hi(4, 1), outputs_hi(), p_hi(5, 1), exps(), p_hi(5, 0), small_half(4), tanh(), hidden_hi(), p_hi(6, 1)
            small_half(5), p_hi(6, 0), outputs_hi(), p_hi(7, 1), p_hi(7, 0), small_half(6), hidden_hi()
            small_half(7), tanh(), outputs_hi(), hidden_hi(), x_hi(xf_t), tanh(), tanh(), hidden_hi(), tanh()
            hidden_hi(), tanh(), hidden_hi(), hidden_hi()

        @block.vector
        def _(dve):
            turn, per_turn = Turn(raised), dict(T=JOBS["T"], Q=JOBS["Q"], S=JOBS["S"], R=JOBS["S"], V=JOBS["V"],
                                         Y=JOBS["Y"], F=JOBS["F"], D=JOBS["D"], LN=JOBS["LN"], X=1, A=1, W=1,
                                         own=DVE_OWN)
            c = tally(**per_turn, T0=0)

            def settle(instruction):
                instruction.then_inc(dve_own, 1)
                c["own"] += 1
                dve.wait_ge(dve_own, turn.at(dve_own, c["own"]))

            def split_lo(i):
                dve.wait_ge(w_hi, turn.at(w_hi, i + 1))
                _, dst, k = pieces[i]
                scale = 1.0 if k is None else gamma_sb[:, k:k + 1]
                nc.vector.scalar_tensor_tensor(out=dst[1], in0=stage(i), scalar=scale, in1=dst[0].bitcast(F32),
                                               op0=ALU.mult, op1=ALU.subtract).then_inc(w_lo, 1)

            def statistics(src):
                for t in range(NT):
                    last = nc.vector.bn_stats(stats[:, t], src[:, t])
                last.then_inc(dve_own, 1)
                c["own"] += 1
                value = turn.apart(dve, dve_own, c["own"])
                if turn.now is not None:
                    dve.wait_ge(eye_in, 16)
                dve.wait_ge(dve_own, value)
                for t in range(NT):
                    last = nc.vector.bn_aggr(mean_var[:, t], stats[:, t])
                settle(last)
                nc.vector.tensor_scalar(power_in[:, 0], mean_var[:, :, 1], EPS, None, ALU.add)
                nc.vector.tensor_copy(power_in[:, 1], mean_var[:, :, 1]).then_inc(ln_var, 1)

            def first_statistics():
                dve.wait_ge(x_loaded, turn.at(x_loaded, 16 * (c["X"] + 1)))
                statistics(x_in)
                c["X"] += 1

            def attention_statistics():
                dve.wait_ge(d_used, turn.at(d_used, c["D"]))
                statistics(x1_next)

            def second_statistics(src):
                dve.wait_ge(y_used, turn.at(y_used, c["Y"]))
                statistics(src)

            def normal_rows(src, unit=False):
                dve.wait_ge(ln_pow, turn.at(ln_pow, c["LN"] + 1))
                dve.wait_ge(t_ready, turn.at(t_ready, c["T"]))
                rstd = power_out[:, 0]
                if unit:
                    settle(nc.vector.scalar_tensor_tensor(
                        out=factor[:], in0=power_out[:, 1], scalar=float(DIM) ** 0.5, in1=rstd,
                        op0=ALU.mult, op1=ALU.mult))
                    settle(nc.vector.tensor_scalar(factor[:], factor[:], NORM_MIN, None, ALU.max))
                    settle(nc.vector.reciprocal(factor[:], factor[:]))
                    settle(nc.vector.scalar_tensor_tensor(
                        out=factor[:], in0=factor[:], scalar=float(DIM) ** 0.5, in1=rstd,
                        op0=ALU.mult, op1=ALU.mult))
                    rstd = factor[:]
                for t in range(NT):
                    last = nc.vector.tensor_scalar(xn[:, t], src[:, t], mean_var[:, t, 0:1], rstd[:, t:t + 1],
                                                   ALU.subtract, ALU.mult)
                last.then_inc(xn_ready, 1)
                c["LN"] += 1

            def lo(dst, src, hi):
                dve.wait_ge(t_hi, turn.at(t_hi, c["T"] + 1))
                nc.vector.tensor_tensor(dst, src, hi.bitcast(F32), ALU.subtract).then_inc(t_lo, 1)
                c["T"] += 1

            def x_lo(dst):
                lo(dst[1][:].rearrange("p k s -> p (k s)"), t_bank(c)[:], dst[0][:].rearrange("p k s -> p (k s)"))

            def q_lo(t, i):
                dve.wait_ge(t_hi, turn.at(t_hi, c["T"] + 1))
                src = t_bank(c)[:].rearrange("p (a s) -> p a s", a=4)
                for odd in range(2):
                    rows, other = slice(DH * odd, DH * odd + DH), slice(DH - DH * odd, 2 * DH - DH * odd)
                    heads = slice(8 * i + odd, 8 * i + 8, 2)
                    last = nc.vector.tensor_tensor(q_t[other, t, heads, :], src[rows],
                                                   q_t[rows, t, heads, :].bitcast(F32), ALU.subtract)
                last.then_inc(t_lo, 1)
                c["T"] += 1

            def k_lo(t):
                lo(k_t[:, :, 1, t * P:t * P + P],
                   t_bank(c)[:].rearrange("p (h s) -> p h s", h=KV_HEADS),
                   k_t[:, :, 0, t * P:t * P + P])

            def p_lo(n, kb):
                lo(p_t[n % 2][1][:, kb], t_bank(c)[:], p_t[n % 2][0][:, kb])

            def rope_products(t, i):
                slot, b = c["Q"] % 2, bank[Q_BANKS[i]]
                heads, half = (8 if i < 2 else KV_HEADS), DH // 2
                src = b[:, 0:heads * DH].rearrange("p (h d) -> p h d", h=heads)
                dve.wait_ge(q_ready, turn.at(q_ready, c["Q"] + 1))
                dve.wait_ge(rope_sum, turn.at(rope_sum, c["Q"] - 1))
                nc.vector.tensor_tensor(rope_c[:, slot, 0:heads], src,
                                        rope_sb[:, t, 0].unsqueeze(1).broadcast_to([P, heads, DH]), ALU.mult)
                for s in range(2):
                    to, of = slice(half * s, half * s + half), slice(half - half * s, DH - half * s)
                    last = nc.vector.tensor_tensor(rope_s[:, slot, 0:heads, to], src[:, :, of],
                                                   rope_sb[:, t, 1, to].unsqueeze(1).broadcast_to([P, heads, half]),
                                                   ALU.mult)
                last.then_inc(rope_mul, 1)
                c["Q"] += 1
                if i == 2:
                    vals = b[:, KV_HEADS * DH:2 * KV_HEADS * DH].rearrange("p (a e d) -> p a e d", a=2, e=2)
                    pair = v_halves[:, t].rearrange("p (a e) (s d) -> p a (e s) d", a=2, s=2)
                    settle(nc.vector.tensor_copy(pair[:, :, 0:4:3], vals))
                    nc.vector.tensor_tensor(pair[:, :, 1:3], vals, pair[:, :, 0:4:3].bitcast(F32), ALU.subtract
                                            ).then_inc(v_done, 1)

            def mask_max(pair):
                slot, keys = c["S"] % 4, P * key_blocks(c["S"] % GROUPS)
                n = c["S"] % GROUPS
                second_tile = n >= KV_HEADS
                semaphore = s_ready if second_tile else low_masked
                count = 2 * c["S"] if second_tile else c["S"] // GROUPS * 2 * KV_HEADS + 2 * n
                value = turn.apart(dve, semaphore, count + pair + 1)
                if turn.now is not None:
                    dve.wait_ge(eye_in, 16)
                dve.wait_ge(semaphore, value)
                for g in range(2 * pair, 2 * pair + 2):
                    part = probs[:, slot, g, 0:keys]
                    last = nc.vector.tensor_tensor_reduce(
                        part, bank[S_BANKS[pair]][:, g % 2 * SEQ:g % 2 * SEQ + keys],
                        mask_sb[:, SEQ - keys:SEQ] if second_tile else part, 1.0, -3.4e38, ALU.add, ALU.max,
                        row_max[:, slot, g:g + 1])
                last.then_inc(s_used, 1)
                if pair:
                    dve.wait_ge(s_used, turn.at(s_used, 2 * c["S"] + 2))
                    nc.vector.tensor_scalar(neg_max[:, slot], row_max[:, slot], -DH ** -0.5, None, ALU.mult
                                            ).then_inc(s_max, 1)
                    c["S"] += 1

            def inverse():
                slot = c["R"] % 4
                dve.wait_ge(e_done, turn.at(e_done, c["R"] + 1))
                nc.vector.reciprocal(inv_sum[:, slot], row_sum[:, slot]).then_inc(r_done, 1)
                c["R"] += 1

            def add_large_half(n):
                rows = slice(DH * (n % 2), DH * (n % 2) + DH)
                dve.wait_ge(o_small, turn.at(o_small, c["V"] + 1))
                nc.vector.tensor_tensor(o_sums[rows], o_sums[rows], bank[O_BANK][rows], ALU.add).then_inc(o_sum, 1)
                c["V"] += 1

            def attention_residual(dst, t):
                dve.wait_ge(y_ready, turn.at(y_ready, c["Y"] + 1))
                dve.wait_ge(x1_kept, turn.at(x1_kept, c["Y"] // NT + 1))
                dve.wait_ge(d_used, turn.at(d_used, c["D"]))
                nc.vector.tensor_tensor(dst[:, t], bank[Y_BANKS[t]][:, 0:DIM], x1[:, t], ALU.add
                                        ).then_inc(y_used, 1)
                c["Y"] += 1

            def gate_product():
                slot = c["F"] % 2
                dve.wait_ge(th_done, turn.at(th_done, c["F"] + 1))
                nc.vector.scalar_tensor_tensor(out=hid[:, slot], in0=hid[:, slot], scalar=1.0, in1=bank[G_BANK][:],
                                               op0=ALU.add, op1=ALU.mult).then_inc(gate_used, 1)

            def up_product():
                slot = c["F"] % 2
                dve.wait_ge(u_ready, turn.at(u_ready, c["F"] + 1))
                dve.wait_ge(gate_used, turn.at(gate_used, c["F"] + 1))
                nc.vector.tensor_tensor(hid[:, slot], hid[:, slot], bank[U_BANK][:], ALU.mult
                                        ).then_inc(mul_done, 1)
                c["F"] += 1

            def ffn_residual(dst, src):
                dve.wait_ge(dn_done, turn.at(dn_done, PAIRS * (c["D"] + 1)))
                if dst is x1_next:
                    dve.wait_ge(x1_kept, turn.at(x1_kept, c["A"]))
                    c["A"] += 1
                else:
                    dve.wait_ge(x_sent, turn.at(x_sent, 16 + 16 * c["W"]))
                    c["W"] += 1
                nc.vector.scalar_tensor_tensor(
                    out=dst[:].rearrange("p t d -> p (t d)"), in0=bank[D_BANK][:], scalar=0.25,
                    in1=src[:].rearrange("p t d -> p (t d)"), op0=ALU.mult, op1=ALU.add
                ).then_inc(d_used, 1)
                c["D"] += 1

            nc.vector.memset(o_sums[:], 0.0).then_inc(zeros_set, 1)

            c["T0"] = -1
            dve.wait_ge(x0_loaded, turn.at(x0_loaded, 16))
            statistics(x2), normal_rows(x2), split_lo(0), x_lo(xf_t), split_lo(1), first_statistics()
            gate_product(), up_product(), split_lo(2), gate_product(), split_lo(3), up_product(), split_lo(6)
            gate_product(), up_product(), split_lo(7), gate_product(), up_product(), normal_rows(x_in), split_lo(8)
            x_lo(xf_t), split_lo(9), ffn_residual(x1_next, x2), attention_statistics(), gate_product(), up_product()
            normal_rows(x1_next, True), x_lo(xa_t), gate_product(), up_product()
            dve.wait_ge(rope_in, turn.at(rope_in, 16))
            rope_products(0, 0), rope_products(0, 1), rope_products(0, 2), rope_products(1, 0), q_lo(0, 0)
            rope_products(1, 1), q_lo(0, 1), k_lo(0), gate_product(), rope_products(1, 2), mask_max(0), mask_max(1)
            q_lo(1, 1), up_product(), mask_max(0), inverse(), mask_max(1), q_lo(1, 0), mask_max(0), mask_max(1)
            k_lo(1), p_lo(0, 0), inverse(), mask_max(0), mask_max(1), inverse(), mask_max(0), mask_max(1)
            add_large_half(0), p_lo(1, 0), mask_max(0), inverse(), mask_max(1), inverse(), add_large_half(1)
            p_lo(2, 0), mask_max(0), mask_max(1), gate_product(), inverse(), mask_max(0), p_lo(3, 0), up_product()
            inverse(), add_large_half(2), p_lo(4, 1), p_lo(4, 0), add_large_half(3), mask_max(1), p_lo(5, 1)
            p_lo(5, 0), inverse(), add_large_half(4), p_lo(6, 1), p_lo(6, 0), ffn_residual(x1_next, x_in)
            add_large_half(5), p_lo(7, 0), attention_statistics(), p_lo(7, 1), add_large_half(6)
            normal_rows(x1_next, True), attention_residual(x2, 0), add_large_half(7), x_lo(xa_t)
            attention_residual(x2, 1)

            before = dict(c)
            with dve.Fori(1, BATCH - 1) as turn.now:
                c["T0"] = c["T"]
                first_statistics(), rope_products(0, 0), rope_products(0, 1), normal_rows(x_in), rope_products(0, 2)
                x_lo(xf_t), rope_products(1, 0), q_lo(0, 0), gate_product(), second_statistics(x2), up_product()
                k_lo(0), q_lo(0, 1), gate_product(), rope_products(1, 1), up_product(), mask_max(0)
                rope_products(1, 2), mask_max(1), gate_product(), up_product(), mask_max(0), normal_rows(x2)
                q_lo(1, 0), mask_max(1), mask_max(0), q_lo(1, 1), inverse(), gate_product(), mask_max(1), inverse()
                x_lo(xf_t), up_product(), mask_max(0), k_lo(1), mask_max(1), inverse(), gate_product(), p_lo(0, 0)
                mask_max(0), inverse(), mask_max(1), p_lo(1, 0), add_large_half(0), mask_max(0), up_product()
                inverse(), mask_max(1), add_large_half(1), p_lo(2, 0), mask_max(0), p_lo(3, 0), gate_product()
                mask_max(1), up_product(), inverse(), add_large_half(2), mask_max(0), p_lo(4, 1), p_lo(4, 0)
                inverse(), ffn_residual(x1_next, x_in), add_large_half(3), mask_max(1), gate_product(), p_lo(5, 1)
                p_lo(5, 0), up_product(), add_large_half(4), inverse(), p_lo(6, 1), gate_product(), p_lo(6, 0)
                add_large_half(5), up_product(), attention_statistics(), p_lo(7, 1), p_lo(7, 0), add_large_half(6)
                normal_rows(x1_next, True), add_large_half(7), x_lo(xa_t), ffn_residual(y_out, x2)
                attention_residual(x2, 0), attention_residual(x2, 1)
            turn.now = None
            after_loop(c, before, per_turn, BATCH - 2)

            c["T0"] = c["T"]
            second_statistics(x2), rope_products(0, 0), rope_products(0, 1), normal_rows(x2), rope_products(0, 2)
            q_lo(0, 0), q_lo(0, 1), rope_products(1, 0), k_lo(0), rope_products(1, 1), x_lo(xf_t), mask_max(0)
            mask_max(1), rope_products(1, 2), mask_max(0), mask_max(1), q_lo(1, 0), inverse(), q_lo(1, 1)
            mask_max(0), inverse(), k_lo(1), mask_max(1), gate_product(), p_lo(0, 0), up_product(), mask_max(0)
            inverse(), mask_max(1), p_lo(1, 0), add_large_half(0), mask_max(0), mask_max(1), inverse(), mask_max(0)
            gate_product(), add_large_half(1), mask_max(1), inverse(), mask_max(0), p_lo(2, 0), mask_max(1)
            p_lo(3, 0), inverse(), mask_max(0), add_large_half(2), mask_max(1), inverse(), p_lo(4, 0)
            add_large_half(3), p_lo(4, 1), up_product(), p_lo(5, 1), inverse(), p_lo(5, 0), add_large_half(4)
            gate_product(), p_lo(6, 1), add_large_half(5), p_lo(6, 0), up_product(), p_lo(7, 1), p_lo(7, 0)
            add_large_half(6), add_large_half(7), attention_residual(x_in, 0), gate_product()
            attention_residual(x_in, 1), second_statistics(x_in), up_product(), normal_rows(x_in), x_lo(xf_t)
            gate_product(), up_product(), ffn_residual(y_out, x2), gate_product(), up_product(), gate_product()
            up_product(), gate_product(), up_product(), ffn_residual(y_out, x_in)

        @block.tensor
        def _(pe):
            turn, per_turn = Turn(raised), dict(T=JOBS["T"], Q=JOBS["Q"], S=JOBS["S"], O=JOBS["V"], Y=JOBS["Y"],
                                        F=JOBS["F"], DN=JOBS["F"], D=JOBS["D"], LN=JOBS["LN"], V=NT,
                                        last0=JOBS["T"], last1=JOBS["T"])
            c = tally(**per_turn, T0=0, P0=0, Q0=0, O0=0, qk0=0, qk1=0, ff=0, xa=0, p0=0, p1=0)

            def product(dst, a, b, start, stop, shared=False):
                for i, (x, y) in enumerate(((0, 0), (0, 1), (1, 0))):
                    last = nc.tensor.matmul(dst, a[x], b[y], start=start and i == 0, stop=stop and i == 2,
                                            skip_group_check=shared)
                return last

            def transposes(blocks):
                last_use = f"last{(c['T'] - c['T0']) % 2}"
                pe.wait_ge(t_lo, turn.at(t_lo, c[last_use]))
                for i, block_in in enumerate(blocks):
                    last = nc.tensor.transpose(t_bank(c)[:, i * P:i * P + P], block_in, eye_sb[:])
                last.then_inc(t_ready, 1)
                c["T"] += 1
                c[last_use] = c["T"]

            def x_transposes(use):
                pe.wait_ge(xn_ready, turn.at(xn_ready, c["LN"] + 1))
                transposes([xn[:, t, k * P:k * P + P] for k in range(KC) for t in range(NT)])
                c["LN"] += 1
                c[use] = c["T"]

            def q_transposes(part, t, i):
                pe.wait_ge(rope_sum, turn.at(rope_sum, c["Q0"] + 3 * t + i + 1))
                if i < 2:
                    transposes([q_rot[:, i, a * P:a * P + P] for a in range(4)])
                else:
                    transposes([k_rot[:, j].rearrange("p c d -> p (c d)") for j in range(KV_HEADS)])
                assert t or TILE0_DONE[part][i] == c["T"] - c["T0"]
                c[f"qk{t}"] = c["T"]

            def qkv(t, i):
                if t == 0 and i == 0:
                    pe.wait_ge(t_lo, turn.at(t_lo, c["xa"]))
                if t == 0 and i < 2:
                    pe.wait_ge(y_used, turn.at(y_used, c["Y"] - 1 + i))
                elif t == 1 and i < 2:
                    pe.wait_ge(rope_mul, turn.at(rope_mul, c["Q"] - 2))
                elif t == 1:
                    pe.wait_ge(v_done, turn.at(v_done, c["V"]))
                rows = slice(t * P, t * P + P)
                for k in range(KC):
                    last = product(bank[Q_BANKS[i]][:], [x[:, k, rows] for x in xa_t],
                                   [w[:, k, 512 * i:512 * i + 512] for w in qkv_w], k == 0, k == KC - 1)
                last.then_inc(q_ready, 1)
                c["Q"] += 1
                c["V"] += i == 2

            def scores(pair):
                n = c["S"] % GROUPS
                t, j = n // KV_HEADS, n % KV_HEADS
                pe.wait_ge(t_lo, turn.at(t_lo, c[f"qk{t}"]))
                if n == 0:
                    pe.wait_ge(rope_mul, turn.at(rope_mul, c["Q0"] + 4 + pair))
                else:
                    pe.wait_ge(s_used, turn.at(s_used, 2 * c["S"] - 1 + pair))
                for g in range(2 * pair, 2 * pair + 2):
                    dst = bank[S_BANKS[pair]][:, g % 2 * SEQ:g % 2 * SEQ + SEQ]
                    if t == 0:
                        last = nc.tensor.matmul(dst, q_t[:, t, KV_HEADS * g + j, :], k_t[:, j, :, 0:P],
                                                start=True, stop=True)
                        continue
                    for s in range(2):
                        last = nc.tensor.matmul(dst, q_t[:, t, KV_HEADS * g + j, :], k_t[:, j, s, :],
                                                start=s == 0, stop=s == 1)
                last.then_inc(s_ready, 1)
                c["S"] += pair

            def p_transposes(n, kb):
                pe.wait_ge(p_done, turn.at(p_done, c["P0"] + n + 1))
                if n == 1:
                    pe.wait_ge(rope_sum, turn.at(rope_sum, c["Q0"] + 6))
                transposes([probs[:, n % 4, g, kb * P:kb * P + P] for g in range(GROUP)])
                c[f"p{n % 2}"] = c["T"]

            def values(n):
                t, j = n // KV_HEADS, n % KV_HEADS
                pe.wait_ge(t_lo, turn.at(t_lo, c[f"p{n % 2}"]))
                if n == 0:
                    pe.wait_ge(v_done, turn.at(v_done, c["V"]))
                else:
                    pe.wait_ge(o_sum, turn.at(o_sum, c["O"]))
                for kb in range(t + 1):
                    for s in range(2):
                        last = nc.tensor.matmul(bank[O_BANK][:], v_halves[:, kb, j], p_t[n % 2][s][:, kb],
                                                start=kb == 0 and s == 0, stop=kb == t and s == 1)
                last.then_inc(o_ready, 1)
                c["O"] += 1

            def projection(t, jp):
                pe.wait_ge(o_lo, turn.at(o_lo, c["O0"] // 2 + 2 * t + jp + 1))
                if jp == 0:
                    pe.wait_ge(s_used, turn.at(s_used, 2 * c["S"]))
                for k in range(jp, OC, 2):
                    last = product(bank[Y_BANKS[t]][:, 0:DIM], [o[:, t, jp, k // 2] for o in o_t],
                                   [w[:, k] for w in out_w], k == 0, k == OC - 1)
                if jp:
                    last.then_inc(y_ready, 1)
                    c["Y"] += 1

            def hidden_product(weight, b):
                for h in range(2):
                    cols = slice((2 * (c["F"] % PAIRS) + h) * P, (2 * (c["F"] % PAIRS) + h + 1) * P)
                    for k in range(KC):
                        last = product(bank[b][:, h * SEQ:h * SEQ + SEQ], [w[:, k, cols] for w in weight],
                                       [x[:, k] for x in xf_t], k == 0, k == KC - 1)
                return last

            def gate():
                pe.wait_ge(t_lo, turn.at(t_lo, c["ff"]))
                pe.wait_ge(gate_used, turn.at(gate_used, c["F"]))
                hidden_product(gate_w, G_BANK).then_inc(g_ready, 1)

            def up():
                pe.wait_ge(mul_done, turn.at(mul_done, c["F"]))
                hidden_product(up_w, U_BANK).then_inc(u_ready, 1)
                c["F"] += 1

            def down():
                p, slot = c["DN"] % PAIRS, c["DN"] % 2
                pe.wait_ge(h_lo, turn.at(h_lo, c["DN"] + 1))
                if p == 0:
                    pe.wait_ge(d_used, turn.at(d_used, c["D"]))
                for t in range(NT):
                    for h in range(2):
                        last = product(bank[D_BANK][:, t * DIM:t * DIM + DIM],
                                       [x[:, slot, h, t * P:t * P + P] for x in (hid_hi, hid_lo)],
                                       [w[:, 2 * p + h] for w in down_w],
                                       p == 0 and t == 0 and h == 0, p == PAIRS - 1 and t == NT - 1 and h == 1,
                                       shared=True)
                last.then_inc(dn_done, 1)
                c["DN"] += 1
                if p == PAIRS - 1:
                    c["D"] += 1

            pe.wait_ge(zeros_set, turn.at(zeros_set, 1))
            for _ in range(3):
                nc.tensor.matmul(bank[G_BANK][:], o_sums[:, 0:P], o_sums[:], start=True, stop=True)

            c["T0"] = -1
            pe.wait_ge(eye_in, turn.at(eye_in, 16))
            x_transposes("ff")
            pe.wait_ge(w_lo, turn.at(w_lo, 1))
            gate()
            pe.wait_ge(w_lo, turn.at(w_lo, 2))
            up(), gate(), up()
            pe.wait_ge(w_lo, turn.at(w_lo, 3))
            gate()
            pe.wait_ge(w_lo_pool, turn.at(w_lo_pool, 1))
            down()
            pe.wait_ge(w_lo, turn.at(w_lo, 4))
            up(), gate(), up(), down(), x_transposes("ff")
            pe.wait_ge(w_lo_pool, turn.at(w_lo_pool, 2))
            down(), down(), gate(), up(), gate(), x_transposes("xa"), up()
            pe.wait_ge(w_lo, turn.at(w_lo, 8))
            qkv(0, 0), qkv(0, 1), qkv(0, 2), qkv(1, 0), q_transposes("opening", 0, 0), qkv(1, 1)
            q_transposes("opening", 0, 1), q_transposes("opening", 0, 2), gate(), qkv(1, 2)
            pe.wait_ge(w_lo_pool, turn.at(w_lo_pool, 4))
            scores(0), scores(1), q_transposes("opening", 1, 1), q_transposes("opening", 1, 0), up(), scores(0)
            scores(1), down(), q_transposes("opening", 1, 2), scores(0), scores(1), gate(), p_transposes(0, 0)
            scores(0), scores(1), down(), values(0), scores(0), scores(1), p_transposes(1, 0), scores(0), scores(1)
            p_transposes(2, 0), values(1), scores(0), scores(1), p_transposes(3, 0), down(), values(2), scores(0)
            up(), scores(1), p_transposes(4, 1), p_transposes(4, 0), values(3), p_transposes(5, 1)
            p_transposes(5, 0), values(4), down(), p_transposes(6, 1), p_transposes(6, 0), values(5)
            p_transposes(7, 0), projection(0, 0), p_transposes(7, 1), values(6), projection(0, 1), values(7)
            projection(1, 0), x_transposes("xa"), projection(1, 1)

            before = dict(c)
            with pe.Fori(1, BATCH - 1) as turn.now:
                c["T0"], c["P0"], c["Q0"], c["O0"], c["xa"] = c["T"], c["S"], c["Q"], c["O"], c["T"]
                qkv(0, 0), qkv(0, 1), qkv(0, 2), qkv(1, 0), x_transposes("ff"), q_transposes("turn", 0, 0)
                qkv(1, 1), gate(), q_transposes("turn", 0, 2), up(), q_transposes("turn", 0, 1), gate(), qkv(1, 2)
                up(), scores(0), q_transposes("turn", 1, 0), gate(), scores(1), down(), scores(0), up(), scores(1)
                q_transposes("turn", 1, 1), gate(), scores(0), up(), x_transposes("ff"), scores(1), down()
                scores(0), q_transposes("turn", 1, 2), down(), scores(1), gate(), p_transposes(0, 0), up()
                scores(0), p_transposes(1, 0), scores(1), values(0), gate(), scores(0), p_transposes(2, 0)
                scores(1), values(1), scores(0), p_transposes(3, 0), up(), scores(1), down(), values(2), scores(0)
                p_transposes(4, 1), p_transposes(4, 0), gate(), scores(1), values(3), up(), p_transposes(5, 1)
                p_transposes(5, 0), down(), values(4), gate(), p_transposes(6, 1), p_transposes(6, 0), up()
                values(5), down(), p_transposes(7, 1), p_transposes(7, 0), values(6), projection(0, 0), down()
                values(7), projection(0, 1), x_transposes("xa"), projection(1, 0), down(), projection(1, 1)
            turn.now = None
            after_loop(c, before, per_turn, BATCH - 2)

            c["T0"], c["P0"], c["Q0"], c["O0"], c["xa"] = c["T"], c["S"], c["Q"], c["O"], c["T"]
            qkv(0, 0), qkv(0, 1), qkv(0, 2), q_transposes("ending", 0, 0), q_transposes("ending", 0, 1), qkv(1, 0)
            q_transposes("ending", 0, 2), qkv(1, 1), x_transposes("ff"), scores(0), scores(1)
            q_transposes("ending", 1, 0), qkv(1, 2), scores(0), scores(1), q_transposes("ending", 1, 1), gate()
            scores(0), scores(1), q_transposes("ending", 1, 2), up(), p_transposes(0, 0), scores(0), scores(1)
            p_transposes(1, 0), gate(), values(0), scores(0), scores(1), p_transposes(2, 0), values(1), scores(0)
            scores(1), up(), p_transposes(3, 0), scores(0), scores(1), values(2), scores(0), scores(1)
            p_transposes(4, 0), p_transposes(4, 1), values(3), gate(), p_transposes(5, 1), projection(0, 0)
            values(4), p_transposes(5, 0), up(), p_transposes(6, 1), values(5), p_transposes(6, 0), gate()
            p_transposes(7, 1), p_transposes(7, 0), values(6), down(), values(7), projection(0, 1), projection(1, 0)
            projection(1, 1), up(), down(), down(), x_transposes("ff"), down(), gate(), up(), gate(), up(), gate()
            up(), down(), gate(), up(), down(), down(), down()


_INS = ["x", "w_gate", "w_up", "w_down", "w_qkv", "w_out", "gamma", "rope", "mask", "eye"]


def _chunks(w):
    return np.ascontiguousarray(w.reshape(w.shape[0] // P, P, w.shape[1]).transpose(1, 0, 2))


def _rope_table():
    inv = np.float32(10000.0) ** -(np.arange(0, DH, 2, dtype=np.float32) / np.float32(DH))
    angle = (np.arange(SEQ, dtype=np.float32)[:, None] * inv[None, :].astype(np.float32)).astype(np.float64)
    cos, sin = np.cos(angle), np.sin(angle)
    table = np.stack([np.concatenate([cos, cos], 1), np.concatenate([-sin, sin], 1)], 1)
    return np.ascontiguousarray(table.reshape(NT, P, 2, DH).transpose(1, 0, 2, 3).astype(np.float32))


def kernel(L0_attn_x, L0_attn_gamma, L0_attn_w_qkv, L0_attn_w_out, L0_ffn_w_gate, L0_ffn_w_up, L0_ffn_w_down):
    import concourse.bacc as _bacc
    from concourse.bass_utils import run_bass_kernel_spmd as _run

    causal = np.where(np.tril(np.ones((P, P), bool)), 0.0, MASKED).astype(np.float32)
    given = {
        "x": np.ascontiguousarray(L0_attn_x),
        "w_gate": _chunks(np.asarray(L0_ffn_w_gate).T),
        "w_up": _chunks(np.asarray(L0_ffn_w_up).T),
        "w_down": _chunks(np.asarray(L0_ffn_w_down).T),
        "w_qkv": _chunks(np.asarray(L0_attn_w_qkv)),
        "w_out": _chunks(np.asarray(L0_attn_w_out)),
        "gamma": np.ascontiguousarray(np.asarray(L0_attn_gamma).reshape(KC, P).T),
        "rope": _rope_table(),
        "mask": np.concatenate([np.zeros((P, SEQ - P), np.float32), causal], 1),
        "eye": np.eye(P, dtype=np.float32),
    }
    nc = _bacc.Bacc("TRN2", target_bir_lowering=False, num_devices=1)
    args = [nc.dram_tensor(f"in_{n}", given[n].shape, F32, kind="ExternalInput").ap() for n in _INS]
    out = nc.dram_tensor("out_0", (BATCH, SEQ, DIM), F32, kind="ExternalOutput").ap()
    build(nc, *args, out)
    r = _run(nc, [{f"in_{n}": given[n] for n in _INS}], core_ids=[0])
    return r.results[0]["out_0"]
```
